# Optimizing a Trainium2 kernel written in Bass

```python
import numpy as np
import jax
import jax.numpy as jnp

def _softmax(x, axis=-1):
    return jax.nn.softmax(x, axis=axis)
def _gelu(x):
    return jax.nn.gelu(x, approximate=True)
def _silu(x):
    return jax.nn.silu(x)
def _sigmoid(x):
    return jax.nn.sigmoid(x)
def _layernorm(x, axis=-1, eps=1e-5):
    m = jnp.mean(x, axis=axis, keepdims=True)
    v = jnp.var(x, axis=axis, keepdims=True)
    return (x - m) / jnp.sqrt(v + eps)
def _scatter_add(tgt, idx, src, axis=0):
    return tgt.at[idx].add(src)
def _segment_sum(src, seg, n):
    return jax.ops.segment_sum(src, seg, n)

kernel_name = 'mk_conv_preact_d1_conv_nhwc1024_a5e183'

def setup_inputs(seed: int = 0):
    np.random.seed(seed)
    _w = jnp.asarray
    def _rec_inputs():
        import jax
        import jax.numpy as jnp
        _gk = jax.random.key(seed)
        x = -0.0002928 + 1 * jax.random.normal(jax.random.fold_in(_gk, 1), (2, 16, 128, 1024), jnp.float32)
        return x
    x = _rec_inputs()
    def _L0_conv_setup():
        import jax, jax.numpy as jnp
        import numpy as np
        EMBED_DIM = 1024
        NUM_HEADS = 16
        LB_HEADS = 8
        LA_HEADS = 8
        HEAD_DIM = EMBED_DIM // NUM_HEADS

        def _masked_attention(xf, Wq, Wk, Wv, lookahead):
            q = jnp.einsum('bnd,hed->bhne', xf, Wq)
            k = jnp.einsum('bnd,hed->bhne', xf, Wk)
            v = jnp.einsum('bnd,hed->bhne', xf, Wv)
            scale = 1.0 / jnp.sqrt(jnp.asarray(q.shape[-1], q.dtype))
            s = jnp.einsum('bhqe,bhke->bhqk', q, k) * scale
            n = s.shape[-1]
            i = jnp.arange(n)
            mask = i[:, None] <= i[None, :] if lookahead else i[:, None] >= i[None, :]
            s = jnp.where(mask, s, jnp.finfo(s.dtype).min)
            p = jax.nn.softmax(s, axis=-1)
            return jnp.einsum('bhqk,bhke->bhqe', p, v)
        key = jax.random.key(seed)
        ks = jax.random.split(key, 8)
        B, T, F, D = (2, 16, 128, EMBED_DIM)

        def xavier(k, shape):
            fan_out, fan_in = (shape[-2], shape[-1])
            lim = float(np.sqrt(6.0 / (fan_in + fan_out)))
            return jax.random.uniform(k, shape, jnp.float32, -lim, lim)
        return {'x': jax.random.normal(ks[0], (B, T, F, D), jnp.float32), 'Wq_lb': xavier(ks[1], (LB_HEADS, HEAD_DIM, D)), 'Wk_lb': xavier(ks[2], (LB_HEADS, HEAD_DIM, D)), 'Wv_lb': xavier(ks[3], (LB_HEADS, HEAD_DIM, D)), 'Wq_la': xavier(ks[4], (LA_HEADS, HEAD_DIM, D)), 'Wk_la': xavier(ks[5], (LA_HEADS, HEAD_DIM, D)), 'Wv_la': xavier(ks[6], (LA_HEADS, HEAD_DIM, D)), 'Wo': xavier(ks[7], (D, D))}
    _L0_conv_all = _L0_conv_setup()
    _L0_conv_in = {k: v for k, v in _L0_conv_all.items() if k in ('Wq_lb', 'Wk_lb', 'Wv_lb', 'Wq_la', 'Wk_la', 'Wv_la', 'Wo', )}
    del _L0_conv_all

    return {
        "x": x,
        "L0_conv_Wq_lb": _L0_conv_in["Wq_lb"],
        "L0_conv_Wk_lb": _L0_conv_in["Wk_lb"],
        "L0_conv_Wv_lb": _L0_conv_in["Wv_lb"],
        "L0_conv_Wq_la": _L0_conv_in["Wq_la"],
        "L0_conv_Wk_la": _L0_conv_in["Wk_la"],
        "L0_conv_Wv_la": _L0_conv_in["Wv_la"],
        "L0_conv_Wo": _L0_conv_in["Wo"],
    }

def reference(x, L0_conv_Wq_lb, L0_conv_Wk_lb, L0_conv_Wv_lb, L0_conv_Wq_la, L0_conv_Wk_la, L0_conv_Wv_la, L0_conv_Wo):
    import jax
    import jax.numpy as jnp
    def _L0_conv_ref(x, Wq_lb, Wk_lb, Wv_lb, Wq_la, Wk_la, Wv_la, Wo):
        import jax, jax.numpy as jnp
        import numpy as np
        EMBED_DIM = 1024
        NUM_HEADS = 16
        LB_HEADS = 8
        LA_HEADS = 8
        HEAD_DIM = EMBED_DIM // NUM_HEADS

        def _masked_attention(xf, Wq, Wk, Wv, lookahead):
            q = jnp.einsum('bnd,hed->bhne', xf, Wq)
            k = jnp.einsum('bnd,hed->bhne', xf, Wk)
            v = jnp.einsum('bnd,hed->bhne', xf, Wv)
            scale = 1.0 / jnp.sqrt(jnp.asarray(q.shape[-1], q.dtype))
            s = jnp.einsum('bhqe,bhke->bhqk', q, k) * scale
            n = s.shape[-1]
            i = jnp.arange(n)
            mask = i[:, None] <= i[None, :] if lookahead else i[:, None] >= i[None, :]
            s = jnp.where(mask, s, jnp.finfo(s.dtype).min)
            p = jax.nn.softmax(s, axis=-1)
            return jnp.einsum('bhqk,bhke->bhqe', p, v)
        B, T, F, D = x.shape
        xf = x.reshape(B, T * F, D)
        o_lb = _masked_attention(xf, Wq_lb, Wk_lb, Wv_lb, lookahead=False)
        o_la = _masked_attention(xf, Wq_la, Wk_la, Wv_la, lookahead=True)
        o = jnp.concatenate([o_lb, o_la], axis=1)
        o = o.reshape(B, T * F, D)
        out = jnp.einsum('bnd,od->bno', o, Wo)
        return out.reshape(B, T, F, D)

    def _gn(v, G=32, eps=1e-5):
        B_, H_, W_, C_ = v.shape
        g = v.reshape(B_, H_, W_, G, C_ // G)
        m = jnp.mean(g, axis=(1, 2, 4), keepdims=True)
        s = jnp.var(g, axis=(1, 2, 4), keepdims=True)
        return ((g - m) / jnp.sqrt(s + eps)).reshape(v.shape)

    def _ln_c(v, eps=1e-6):
        m = jnp.mean(v, axis=-1, keepdims=True)
        s = jnp.var(v, axis=-1, keepdims=True)
        return (v - m) / jnp.sqrt(s + eps)

    def _ln_t(v, eps=1e-5):
        m = jnp.mean(v, axis=-1, keepdims=True)
        s = jnp.var(v, axis=-1, keepdims=True)
        return (v - m) / jnp.sqrt(s + eps)

    def _to_tokens(v):
        B_, H_, W_, C_ = v.shape
        return v.reshape(B_, H_ * W_, C_)
    def _from_tokens(t, like):
        return t.reshape(like.shape)

    x = x + _L0_conv_ref(_gn(x), L0_conv_Wq_lb, L0_conv_Wk_lb, L0_conv_Wv_lb, L0_conv_Wq_la, L0_conv_Wk_la, L0_conv_Wv_la, L0_conv_Wo)
    return x


_drawn_inputs = setup_inputs


def setup_inputs(seed=0):
    import zlib

    import numpy as np

    out = dict(_drawn_inputs(seed))
    spreads = {}
    factors = {}
    for name, (base, spread) in spreads.items():
        noise = np.random.default_rng([zlib.crc32(name.encode()), seed]).standard_normal(out[name].shape)
        drawn = base * np.exp(spread * noise) if base else spread * noise
        out[name] = jnp.asarray(drawn.astype(out[name].dtype))
    for name, factor in factors.items():
        out[name] = (out[name] * factor).astype(out[name].dtype)
    return out
```

```python
from contextlib import ExitStack

import concourse.bass as bass
from concourse import mybir

F32 = mybir.dt.float32
F32R = mybir.dt.float32r
BF16 = mybir.dt.bfloat16
ALU = mybir.AluOpType
ACT = mybir.ActivationFunctionType
AX = mybir.AxisListType

P = 128
B = 2
T = 2048
D = 1024
E = 64
HEADS = 8
KINDS = 2
LB, LA = 0, 1
G_HEADS = KINDS * B * HEADS
NC = D // P
NQ = 512
GROUP = 32
GN_EPS = 1e-5
SCALE = float(E) ** -0.5
MASKED = -1.0e30



def reached(eng, sem, value):
    if isinstance(value, int) and value <= 0:
        return
    eng.wait_ge(sem, value)



BLOCKS = 16
PAIR_BLOCKS = 8
V_RAWS = 4
TOK = T // P
TILES_KIND = PAIR_BLOCKS * (T // NQ) + TOK
RAWS_KIND = PAIR_BLOCKS + V_RAWS


def project(nc, xT, wqk, wv, qk_s, v_s):
    with ExitStack() as ctx:
        def sb(name, shape, dt=F32):
            return ctx.enter_context(nc.sbuf_tensor(name, shape, dt))

        def sem(name):
            return ctx.enter_context(nc.semaphore(name))

        xh = sb("xh", [P, NC, T], F32R)
        xl = sb("xl", [P, NC, T], F32R)
        xs = sb("xs", [P, 2, T])
        w_raw = sb("w_raw", [P, D])
        wh = sb("wh", [P, 2, NC, P], F32R)
        wl = sb("wl", [P, 2, NC, P], F32R)
        vh = sb("vh", [P, NC, NQ], F32R)
        vl = sb("vl", [P, NC, NQ], F32R)
        stage_a = sb("stage_a", [P, 2, NQ])
        stage_d = sb("stage_d", [P, 2, NQ])
        average = sb("average", [P, P])
        stats = sb("stats", [P, 2, T // NQ, 6])
        channel = sb("channel", [P, 2, 2])
        centre = sb("centre", [P, 2, 1])
        spread = sb("spread", [P, 2, 1])
        group_mean = sb("group_mean", [P, 2, 1])
        group_var = sb("group_var", [P, 2, 1])
        deviation = sb("deviation", [P, 2, 1])
        inverse = sb("inverse", [P, 2, 1])
        bank = [ctx.enter_context(nc.psum_tensor(f"proj{n}", [P, NQ], F32)) for n in range(8)]

        x_loaded = [sem(f"x_loaded{n}") for n in range(2)]
        w_loaded = sem("w_loaded")
        average_ready = sem("average_ready")
        dve_step = sem("dve_step")
        channel_ready = sem("channel_ready")
        mean_summed = sem("mean_summed")
        spread_ready = sem("spread_ready")
        var_summed = sem("var_summed")
        var_ready = sem("var_ready")
        deviation_ready = sem("deviation_ready")
        x_normal = sem("x_normal")
        x_high = sem("x_high")
        x_low = sem("x_low")
        w_high = sem("w_high")
        w_low = sem("w_low")
        tile_done = sem("tile_done")
        out_a = sem("out_a")
        out_d = sem("out_d")
        stored_a = [sem(f"stored_a{n}") for n in range(2)]
        stored_d = [sem(f"stored_d{n}") for n in range(2)]

        def blocks(eng, final, body):
            for u in range(2):
                body(u, u, True)
            turns = PAIR_BLOCKS // 2 - final
            with eng.Fori(1, turns) as m:
                for u in range(2):
                    body(2 * m + u, u, True)
            if final:
                for u in range(2):
                    body(2 * turns + u, u, u == 0)

        def tile(b, kind, t):
            return (b * KINDS + kind) * TILES_KIND + t

        def raw(b, kind, r):
            return (b * KINDS + kind) * RAWS_KIND + r

        V_TILES = PAIR_BLOCKS * (T // NQ)

        block = ctx.enter_context(nc.Block())

        @block.sync
        def _(sp):
            def load_w(src, r):
                reached(sp, w_low, r)
                sp.dma_start(w_raw[:, :], src).then_inc(w_loaded, 16)

            def load_x(n):
                reached(sp, x_low, n - 1)
                sp.dma_start(xs[:, n % 2, :], xT[n // NC, n % NC]).then_inc(x_loaded[n % 2], 16)

            def store(dst, t, n):
                done, stage, stored = ((out_a, stage_a, stored_a), (out_d, stage_d, stored_d))[t % 2]
                slot = (t // 2) % 2
                sp.wait_ge(done, n // 2 + 1)
                sp.dma_start(dst, stage[:, slot, :]).then_inc(stored[slot], 16)

            load_w(wqk[0], 0)
            for b in range(B):
                for c in range(NC):
                    load_x(b * NC + c)
                for kind in range(KINDS):
                    for r in range(V_RAWS):
                        load_w(wv[kind, r], raw(b, kind, 1 + r))

                    def one(n, u, more, b=b, kind=kind):
                        if more:
                            following = (n + (kind * PAIR_BLOCKS + 1)) % BLOCKS
                            load_w(wqk[bass.ds(following, 1)].rearrange("a p d -> (a p) d"),
                                   n + raw(b, kind, V_RAWS + 1))
                        row = n // 4 * (B * 4) + n % 4 + (kind * 2 * B + b) * 4
                        for q in range(T // NQ):
                            store(qk_s[bass.ds(row, 1), :, q * NQ:(q + 1) * NQ].rearrange("a p t -> (a p) t"),
                                  4 * u + q, n * 4 + tile(b, kind, q))

                    blocks(sp, b == B - 1 and kind == KINDS - 1, one)
                    for t in range(TOK):
                        heads = v_s[(kind * B + b) * HEADS:(kind * B + b + 1) * HEADS, :, t, :]
                        store(heads.rearrange("h p e -> p h e"), t, tile(b, kind, V_TILES + t))
            for s in (*stored_a, *stored_d):
                sp.wait_ge(s, 16 * (B * KINDS * TILES_KIND // 4))

        @block.gpsimd
        def _(pool):
            for n in range(B * NC):
                pool.wait_ge(x_high, n + 1)
                nc.gpsimd.tensor_tensor(xl[:, n % NC, :], xs[:, n % 2, :], xh[:, n % NC, :].bitcast(F32),
                                        ALU.subtract).then_inc(x_low, 1)

        @block.tensor
        def _(pe):
            def stat_mean(n):
                pe.wait_ge(channel_ready, n + 1)
                nc.tensor.matmul(bank[6][:, 0:1], average[:, :], channel[:, n % 2, 0:1],
                                 start=True, stop=True).then_inc(mean_summed, 1)

            def stat_var(n):
                pe.wait_ge(spread_ready, n + 1)
                nc.tensor.matmul(bank[7][:, 0:1], average[:, :], spread[:, n % 2, :],
                                 start=True, stop=True).then_inc(var_summed, 1)

            pe.wait_ge(average_ready, 5)
            for b in range(B):
                reached(pe, out_a, tile(b, 0, 0) // 2)
                reached(pe, out_d, tile(b, 0, 0) // 2)
                for c in range(NC):
                    stat_mean(b * NC + c)
                    stat_var(b * NC + c)
                pe.wait_ge(x_low, (b + 1) * NC)
                pe.wait_ge(var_ready, (b + 1) * NC)

                for kind in range(KINDS):
                    def one(n, u, more, b=b, kind=kind):
                        first = isinstance(n, int) and n == 0
                        pe.wait_ge(w_low, raw(b, kind, 1) if first else n + raw(b, kind, V_RAWS + 1))
                        for q in range(T // NQ):
                            reached(pe, (out_a, out_d)[q % 2], n * 2 + (tile(b, kind, q) // 2 - 3))
                            cols = slice(q * NQ, (q + 1) * NQ)
                            for c in range(NC):
                                for w, x in ((wh, xh), (wh, xl), (wl, xh)):
                                    last = nc.tensor.matmul(
                                        bank[4 * u + q][:, :], w[:, u, c, :], x[:, c, cols],
                                        start=(c == 0 and w is wh and x is xh),
                                        stop=(c == NC - 1 and w is wl))
                            last.then_inc(tile_done, 1)

                    blocks(pe, b == B - 1 and kind == KINDS - 1, one)
                    for t in range(TOK):
                        pe.wait_ge((out_a, out_d)[t % 2], tile(b, kind, V_TILES + t) // 2 - 3)
                        cols = slice(t * P, (t + 1) * P)
                        for c in range(NC):
                            for x, w in ((xh, vh), (xh, vl), (xl, vh)):
                                last = nc.tensor.matmul(bank[t % 8][:, :], x[:, c, cols], w[:, c, :],
                                                        start=(c == 0 and x is xh and w is vh),
                                                        stop=(c == NC - 1 and x is xl))
                        last.then_inc(tile_done, 1)

        def split_block(eng, high, u, r, freed):
            reached(eng, tile_done, freed)
            if high:
                eng.wait_ge(w_loaded, r * 16 + 16)
                eng.activation(wh[:, u, :, :], w_raw[:, :].rearrange("p (c e) -> p c e", c=NC),
                               ACT.Copy).then_inc(w_high, 1)
            else:
                eng.wait_ge(w_high, r + 1)
                eng.tensor_tensor(wl[:, u, :, :], w_raw[:, :].rearrange("p (c e) -> p c e", c=NC),
                                  wh[:, u, :, :].bitcast(F32), ALU.subtract).then_inc(w_low, 1)

        def split_v(eng, high, b, kind):
            reached(eng, tile_done, tile(b, kind, 0))
            for k in range(V_RAWS):
                r = raw(b, kind, 1 + k)
                cs = slice(2 * k, 2 * k + 2)
                src = w_raw[:, :].rearrange("p (c e) -> p c e", c=2)
                if high:
                    eng.wait_ge(w_loaded, 16 * (r + 1))
                    eng.activation(vh[:, cs, :], src, ACT.Copy).then_inc(w_high, 1)
                else:
                    eng.wait_ge(w_high, r + 1)
                    eng.tensor_tensor(vl[:, cs, :], src, vh[:, cs, :].bitcast(F32),
                                      ALU.subtract).then_inc(w_low, 1)

        def copy_out(eng, t, n, stage, stored, done, copy):
            slot = (t // 2) % 2
            eng.wait_ge(tile_done, n + 1)
            count = n // 4 * 16
            reached(eng, stored[slot], count)
            copy(stage[:, slot, :], bank[t % 8][:, :]).then_inc(done, 1)

        def weights_and_tiles(eng, high, b):
            stage, stored, done = (stage_a, stored_a, out_a) if high else (stage_d, stored_d, out_d)
            copy = eng.copy if high else eng.tensor_copy
            odd = 0 if high else 1
            for kind in range(KINDS):
                split_v(eng, high, b, kind)

                def one(n, u, more, b=b, kind=kind):
                    if more:
                        split_block(eng, high, 1 - u, n + raw(b, kind, V_RAWS + 1),
                                    n * 4 + tile(b, kind, 0))
                    for q in range(odd, T // NQ, 2):
                        copy_out(eng, 4 * u + q, n * 4 + tile(b, kind, q), stage, stored, done, copy)

                blocks(eng, b == B - 1 and kind == KINDS - 1, one)
                for t in range(odd, TOK, 2):
                    copy_out(eng, t, tile(b, kind, V_TILES + t), stage, stored, done, copy)

        @block.scalar
        def _(act):
            split_block(act, True, 0, 0, 0)
            for b in range(B):
                for c in range(NC):
                    n = b * NC + c
                    act.wait_ge(var_ready, n + 1)
                    nc.scalar.activation(deviation[:, n % 2, :], group_var[:, n % 2, :],
                                         ACT.Sqrt).then_inc(deviation_ready, 1)
                    act.wait_ge(x_normal, n + 1)
                    nc.scalar.activation(xh[:, c, :], xs[:, n % 2, :], ACT.Copy).then_inc(x_high, 1)
                weights_and_tiles(act, True, b)

        @block.vector
        def _(dve):
            nc.vector.memset(average[:, :], 0.0).then_inc(average_ready, 1)
            dve.wait_ge(average_ready, 1)
            for k in range(P // GROUP):
                part = slice(k * GROUP, (k + 1) * GROUP)
                nc.vector.memset(average[part, part], 1.0 / GROUP).then_inc(average_ready, 1)

            split_block(dve, False, 0, 0, 0)
            steps = [0]

            def step(ins):
                steps[0] += 1
                ins.then_inc(dve_step, 1)
                dve.wait_ge(dve_step, steps[0])

            def stats_of(n):
                dve.wait_ge(x_loaded[n % 2], 16 * (n // 2 + 1))
                for q in range(T // NQ):
                    last = nc.vector.bn_stats(stats[:, n % 2, q, :], xs[:, n % 2, q * NQ:(q + 1) * NQ])
                step(last)
                nc.vector.bn_aggr(channel[:, n % 2, :], stats[:, n % 2, :, :]).then_inc(channel_ready, 1)

            for b in range(B):
                stats_of(b * NC)
                reached(dve, tile_done, tile(b, 0, 0))
                for c in range(NC):
                    n, k = b * NC + c, (b * NC + c) % 2
                    if c + 1 < NC:
                        stats_of(n + 1)
                    dve.wait_ge(mean_summed, n + 1)
                    step(nc.vector.tensor_copy(group_mean[:, k, :], bank[6][:, 0:1]))
                    dve.wait_ge(channel_ready, n + 1)
                    step(nc.vector.tensor_tensor(centre[:, k, :], channel[:, k, 0:1], group_mean[:, k, :],
                                                 ALU.subtract))
                    nc.vector.scalar_tensor_tensor(
                        out=spread[:, k, :], in0=centre[:, k, :], scalar=centre[:, k, 0:1],
                        in1=channel[:, k, 1:2], op0=ALU.mult, op1=ALU.add).then_inc(spread_ready, 1)
                    dve.wait_ge(var_summed, n + 1)
                    nc.vector.tensor_scalar(group_var[:, k, :], bank[7][:, 0:1], GN_EPS, None,
                                            ALU.add).then_inc(var_ready, 1)
                    dve.wait_ge(deviation_ready, n + 1)
                    step(nc.vector.reciprocal(inverse[:, k, :], deviation[:, k, :]))
                    nc.vector.tensor_scalar(xs[:, k, :], xs[:, k, :], group_mean[:, k, 0:1],
                                            inverse[:, k, 0:1], ALU.subtract,
                                            ALU.mult).then_inc(x_normal, 1)
                weights_and_tiles(dve, False, b)



STAGES = T // NQ
S_TILES = 40
M_UNITS = 40
AHEAD = 3
M_AHEAD = 22
PAIRS = G_HEADS // 2
RAW_UNITS = 5
HALF = T // 2
RR = T // 16
JP = 8
OP_PIECES = 6
CR_SLOT = {2: 3, 3: 19, 0: 23, 1: 31}
PREP_SLOT = {0: 1, 1: 3, 2: 5, 3: 8, 4: 10}
ROUND_SLOT = 1
OP_SLOT = {0: 7, 1: 8, 2: 9, 3: 12, 4: 13, 5: 14}


def score_tile(kind, t):
    s = 0
    while t >= 4 * (s + 1):
        t -= 4 * (s + 1)
        s += 1
    over = t - 4 * s
    qb, j = (s, t) if kind == LB else (STAGES - 1 - s, TOK - 1 - t)
    if over < 0:
        return s, t, qb, j, 0, NQ, None
    if kind == LB:
        return s, t, qb, j, over * P, NQ - over * P, over * P
    return s, t, qb, j, 0, NQ - over * P, NQ - (over + 1) * P


def max_unit(kind, n):
    s = 0
    while n >= 4 * (s + 1):
        n -= 4 * (s + 1)
        s += 1
    r, m = n // (s + 1), n % (s + 1)
    keys = (4 * s + r + 1) * P
    lo, hi = m * NQ, min(keys, (m + 1) * NQ)
    diagonal = keys - P if hi == keys else None
    if kind == LB:
        return s, r, m, 4 * s + r, lo, hi - lo, diagonal
    return (s, r, m, TOK - 1 - 4 * s - r, T - hi, hi - lo,
            None if diagonal is None else T - keys)


def slots(has_next, has_before):
    plan = []
    for t in range(S_TILES):
        def add(step, n):
            later = n >= 40
            if has_next or not later:
                plan.append((step, later, n % 40))
        add("scores", t + AHEAD)
        add("max", t + M_AHEAD)
        for s, at in CR_SLOT.items():
            if at == t and (has_next or s >= 2):
                plan.append(("shift", s < 2, s))
        if t == ROUND_SLOT and has_before:
            plan.append(("round", False, 0))
        for u, at in PREP_SLOT.items():
            if at == t and has_next:
                plan.append(("split", True, u))
        for n, at in OP_SLOT.items():
            if at == t and has_before:
                plan.append(("project", False, n))
        plan.append(("values", False, t))
    return plan


def prologue():
    return ([("split", False, u) for u in range(RAW_UNITS)]
            + [("max", False, n) for n in range(4)] + [("shift", False, 0)]
            + [("max", False, n) for n in range(4, 12)] + [("shift", False, 1)]
            + [("max", False, n) for n in range(12, M_AHEAD)]
            + [("scores", False, t) for t in range(AHEAD)])


def attend(nc, x_res, wo, qk_s, v_s, out):
    with ExitStack() as ctx:
        def sb(name, shape, dt=F32):
            return ctx.enter_context(nc.sbuf_tensor(name, shape, dt))

        def sem(name):
            return ctx.enter_context(nc.semaphore(name))

        q1 = sb("q1", [P, 2, T], F32R)
        q2 = sb("q2", [P, 2, T], F32R)
        k1 = sb("k1", [P, 2, T], F32R)
        k2 = sb("k2", [P, 2, T], F32R)
        VC = 3 * E + 1
        v = sb("v", [P, 2, TOK, VC], F32R)
        raw = sb("raw", [P, 2, HALF])
        probs = sb("probs", [P, 4, NQ])
        p_high = sb("p_high", [P, 4, NQ], F32R)
        p_low = sb("p_low", [P, 4, NQ], F32R)
        acc_s = sb("acc_s", [P, NQ])
        inv = sb("inv", [E, NQ])
        o_full = sb("o_full", [P, JP, RR])
        o_high = sb("o_high", [P, JP, RR], F32R)
        o_low = sb("o_low", [P, JP, RR], F32R)
        wo_h = sb("wo_h", [P, JP, D], F32R)
        wo_l = sb("wo_l", [P, JP, D], F32R)
        res = sb("res", [P, 2, NQ])
        part_max = sb("part_max", [P, 2, 4, 4])
        minus_max = sb("minus_max", [P, 2, 4], F32R)
        eye = sb("eye", [P, P])
        eye_r = sb("eye_r", [P, P], F32R)
        eye_b = sb("eye_b", [P, P], BF16)
        below = sb("below", [P, P], BF16)
        beyond = sb("beyond", [P, P], BF16)

        def bank(name):
            return ctx.enter_context(nc.psum_tensor(name, [P, NQ], F32))

        scores = [bank(f"scores{n}") for n in range(4)]
        max_bank = [bank(f"max{n}") for n in range(2)]
        acc = bank("acc")
        side = bank("side")

        raw_loaded = [sem(f"raw_loaded{n}") for n in range(2)]
        wo_loaded = sem("wo_loaded")
        wo_high = sem("wo_high")
        wo_split = sem("wo_split")
        res_loaded = sem("res_loaded")
        cleared = sem("cleared")
        eye_made = sem("eye_made")
        consts = sem("consts")
        act_split = sem("act_split")
        pool_split = sem("pool_split")
        max_scored = sem("max_scored")
        max_read = sem("max_read")
        max_ready = sem("max_ready")
        row_ready = sem("row_ready")
        shift_ready = sem("shift_ready")
        scored = sem("scored")
        exp_done = sem("exp_done")
        high_act = sem("high_act")
        high_dve = sem("high_dve")
        low_pool = sem("low_pool")
        low_dve = sem("low_dve")
        weighed = sem("weighed")
        acc_copied = sem("acc_copied")
        inv_ready = sem("inv_ready")
        o_ready = sem("o_ready")
        o_high_ready = sem("o_high_ready")
        o_low_ready = sem("o_low_ready")
        projected = sem("projected")
        added = sem("added")
        stored = sem("stored")

        def pairs(eng, body):
            body(0, LB, LB)
            with eng.Fori(1, PAIRS // 2 - 1) as i:
                body(i, LB, LB)
            body(PAIRS // 2 - 1, LB, LA)
            with eng.Fori(PAIRS // 2, PAIRS - 1) as i:
                body(i, LA, LA)
            body(PAIRS - 1, LA, None)

        def heads(eng, do):
            for step, _, n in prologue():
                do(step, LB, 0, 0, n)

            def pair(i, kind, then):
                for p in range(2):
                    of = kind if p == 0 else then
                    following = (i, 1) if p == 0 else (i + 1, 0)
                    has_before = p == 1 or not isinstance(i, int) or i > 0
                    for step, later, n in slots(of is not None, has_before):
                        if later:
                            do(step, of, *following, n)
                        else:
                            do(step, kind, i, p, n)

            pairs(eng, pair)
            do("round", None, PAIRS, 0, 0)
            for n in range(OP_PIECES):
                do("project", None, PAIRS, 0, n)

        def count(i, p, per_head, n):
            return i * (2 * per_head) + (p * per_head + n)

        def wait_exp(eng, i, p, t):
            reached(eng, exp_done, count(i, p, S_TILES, t + 1))

        def wait_high(eng, i, p, t):
            reached(eng, (high_dve, high_act)[t % 2], count(i, p, S_TILES // 2, t // 2 + 1))

        def wait_low(eng, i, p, t):
            if t % 4 == 3:
                reached(eng, low_dve, count(i, p, S_TILES // 4, t // 4 + 1))
            else:
                reached(eng, low_pool, count(i, p, S_TILES // 4 * 3, t // 4 * 3 + t % 4 + 1))

        block = ctx.enter_context(nc.Block())

        @block.sync
        def _(sp):
            def load_raw(i, p, kind):
                row = i + kind * PAIRS // 2
                for u in range(RAW_UNITS):
                    slot = (p * RAW_UNITS + u) % 2
                    k = count(i, p, RAW_UNITS, u - 1)
                    reached(sp, act_split, k)
                    reached(sp, pool_split, k)
                    if u < 4:
                        src = qk_s[bass.ds(row + (u // 2) * (B * 4), 1), p * E:(p + 1) * E,
                                   (u % 2) * HALF:(u % 2 + 1) * HALF].rearrange("a e t -> (a e) t")
                        for copy in range(2):
                            sp.dma_start(raw[copy * E:(copy + 1) * E, slot, :], src).then_inc(raw_loaded[slot], 16)
                    else:
                        src = v_s[bass.ds(2 * i + p, 1)].rearrange("a p t e -> (a p) (t e)")
                        for half in range(2):
                            cols = slice(half * NQ, (half + 1) * NQ)
                            sp.dma_start(raw[:, slot, cols], src[:, cols]).then_inc(raw_loaded[slot], 16)

            def residual(g):
                reached(sp, stored, g * 16)
                sp.dma_start(res[:, :, :].rearrange("p a n -> p (a n)"),
                             x_res[bass.ds(g, 1)].rearrange("a p d -> (a p) d")).then_inc(res_loaded, 16)

            def rows_out(g):
                sp.wait_ge(added, g * 2 + 2)
                sp.dma_start(out[bass.ds(g, 1)].rearrange("a p d -> (a p) d"),
                             res[:, :, :].rearrange("p a n -> p (a n)")).then_inc(stored, 16)

            for k in range(JP):
                reached(sp, wo_split, k)
                sp.dma_start(o_full[:, :, :].rearrange("p j r -> p (j r)"), wo[:, k, :]).then_inc(wo_loaded, 16)
            load_raw(0, 0, LB)
            residual(0)

            def pair(i, kind, then):
                for p in range(2):
                    of = kind if p == 0 else then
                    if of is not None:
                        load_raw(*((i, 1) if p == 0 else (i + 1, 0)), of)
                    if p == 1 or not isinstance(i, int) or i > 0:
                        before = 2 * i + (p - 1)
                        rows_out(before)
                        residual(before + 1)

            pairs(sp, pair)
            rows_out(G_HEADS - 1)
            sp.wait_ge(stored, 16 * G_HEADS)

        @block.gpsimd
        def _(pool):
            nc.gpsimd.memset(eye[:, :], 0.0).then_inc(eye_made, 1)
            nc.gpsimd.memset(below[:, :], 0.0).then_inc(eye_made, 1)
            nc.gpsimd.memset(beyond[:, :], 0.0).then_inc(eye_made, 1)
            pool.wait_ge(eye_made, 3)
            nc.gpsimd.affine_select(out=eye[:, :], in_=eye[:, :], compare_op=ALU.not_equal, fill=1.0,
                                    base=0, pattern=[[-1, P]], channel_multiplier=1).then_inc(eye_made, 1)
            nc.gpsimd.affine_select(out=below[:, :], in_=below[:, :], compare_op=ALU.is_ge, fill=MASKED,
                                    base=0, pattern=[[1, P]], channel_multiplier=-1).then_inc(consts, 1)
            nc.gpsimd.affine_select(out=beyond[:, :], in_=beyond[:, :], compare_op=ALU.is_ge, fill=MASKED,
                                    base=0, pattern=[[-1, P]], channel_multiplier=1).then_inc(consts, 1)

            def do(step, kind, i, p, n):
                if step == "split":
                    slot = (p * RAW_UNITS + n) % 2
                    pool.wait_ge(act_split, count(i, p, RAW_UNITS, n + 1))
                    before = PREP_SLOT[n] + AHEAD
                    wait_low(pool, i, p, before - (before % 4 == 3) - S_TILES)
                    cols = slice((n % 2) * HALF, (n % 2 + 1) * HALF)
                    if n < 2:
                        ins = nc.gpsimd.tensor_tensor(q2[0:E, p, cols], raw[0:E, slot, :],
                                                      q1[0:E, p, cols].bitcast(F32), ALU.subtract)
                    elif n < 4:
                        low = k1[E:P, p, cols]
                        ins = nc.gpsimd.tensor_tensor(low, raw[E:P, slot, :], low.bitcast(F32), ALU.subtract)
                    else:
                        ins = nc.gpsimd.tensor_tensor(
                            v[:, p, :, 2 * E:3 * E], raw[:, slot, :].rearrange("p (t e) -> p t e", e=E),
                            v[:, p, :, 0:E].bitcast(F32), ALU.subtract)
                    ins.then_inc(pool_split, 1)
                    pool.wait_ge(pool_split, count(i, p, RAW_UNITS, n + 1))
                elif step == "scores" and n % 4 != 3:
                    wait_high(pool, i, p, n)
                    cols = score_tile(kind, n)[5]
                    reached(pool, weighed, count(i, p, S_TILES, n - 3))
                    nc.gpsimd.tensor_tensor(p_low[:, n % 4, 0:cols], probs[:, n % 4, 0:cols],
                                            p_high[:, n % 4, 0:cols].bitcast(F32),
                                            ALU.subtract).then_inc(low_pool, 1)
                elif step == "round":
                    pool.wait_ge(o_high_ready, count(i, p, 1, 0))
                    nc.gpsimd.tensor_tensor(o_low[:, :, :], o_full[:, :, :], o_high[:, :, :].bitcast(F32),
                                            ALU.subtract).then_inc(o_low_ready, 1)

            heads(pool, do)

        @block.scalar
        def _(act):
            for k in range(JP):
                act.wait_ge(wo_loaded, 16 * (k + 1))
                nc.scalar.activation(wo_h[:, k, :], o_full[:, :, :].rearrange("p j r -> p (j r)"),
                                     ACT.Copy).then_inc(wo_high, 1)

            def do(step, kind, i, p, n):
                if step == "split":
                    slot = (p * RAW_UNITS + n) % 2
                    act.wait_ge(raw_loaded[slot], 32 * (i * RAW_UNITS + ((p * RAW_UNITS + n) // 2 + 1)))
                    reached(act, weighed, count(i, p, S_TILES, -S_TILES))
                    cols = slice((n % 2) * HALF, (n % 2 + 1) * HALF)
                    if n < 2:
                        ins = nc.scalar.activation(q1[:, p, cols], raw[:, slot, :], ACT.Copy)
                    elif n < 4:
                        nc.scalar.activation(k2[0:E, p, cols], raw[0:E, slot, :], ACT.Copy)
                        ins = nc.scalar.activation(k1[:, p, cols], raw[:, slot, :], ACT.Copy)
                    else:
                        ins = nc.scalar.activation(v[:, p, :, 0:E],
                                                   raw[:, slot, :].rearrange("p (t e) -> p t e", e=E), ACT.Copy)
                    ins.then_inc(act_split, 1)
                elif step == "shift":
                    act.wait_ge(row_ready, count(i, p, STAGES, n + 1))
                    qb = n if kind == LB else STAGES - 1 - n
                    nc.scalar.activation(q2[E:E + 1, p, qb * NQ:(qb + 1) * NQ], side[E:E + 1, :],
                                         ACT.Copy).then_inc(shift_ready, 1)
                elif step == "scores":
                    cols = score_tile(kind, n)[5]
                    act.wait_ge(scored, count(i, p, S_TILES, n + 1))
                    wait_low(act, i, p, n - 4)
                    nc.scalar.activation(probs[:, n % 4, 0:cols], scores[n % 4][:, 0:cols], ACT.Exp,
                                         scale=SCALE).then_inc(exp_done, 1)
                    if n % 2:
                        reached(act, weighed, count(i, p, S_TILES, n - 3))
                        nc.scalar.activation(p_high[:, n % 4, 0:cols], scores[n % 4][:, 0:cols], ACT.Exp,
                                             scale=SCALE).then_inc(high_act, 1)
                elif step == "values":
                    s, at = score_tile(kind, n)[:2]
                    if at == 4 * (s + 1) - 1:
                        act.wait_ge(weighed, count(i, p, S_TILES, n + 1))
                        reached(act, o_ready, count(i, p, STAGES, s))
                        nc.scalar.activation(acc_s[:, :], acc[:, :], ACT.Copy).then_inc(acc_copied, 1)
                elif step == "round":
                    act.wait_ge(o_ready, count(i, p, STAGES, 0))
                    reached(act, projected, count(i, p, 2, -2))
                    nc.scalar.activation(o_high[:, :, :], o_full[:, :, :], ACT.Copy).then_inc(o_high_ready, 1)

            heads(act, do)

        @block.vector
        def _(dve):
            for p in range(2):
                nc.vector.memset(q2[E:P, p, :].bitcast(F32), 0.0).then_inc(cleared, 1)
                nc.vector.memset(k2[E:P, p, :].bitcast(F32), 0.0).then_inc(cleared, 1)
                nc.vector.memset(v[:, p, :, E:2 * E].bitcast(F32), 1.0).then_inc(cleared, 1)
                nc.vector.memset(v[:, p, :, 3 * E:VC].bitcast(F32), 0.0).then_inc(cleared, 1)
            dve.wait_ge(cleared, 8)
            for p in range(2):
                nc.vector.memset(k2[E:E + 1, p, :].bitcast(F32), 1.0).then_inc(cleared, 1)
            dve.wait_ge(eye_made, 4)
            nc.vector.tensor_copy(eye_r[:, :], eye[:, :]).then_inc(consts, 1)
            nc.vector.tensor_copy(eye_b[:, :], eye[:, :]).then_inc(consts, 1)
            for k in range(JP):
                dve.wait_ge(wo_high, k + 1)
                nc.vector.tensor_tensor(wo_l[:, k, :], o_full[:, :, :].rearrange("p j r -> p (j r)"),
                                        wo_h[:, k, :].bitcast(F32), ALU.subtract).then_inc(wo_split, 1)

            def do(step, kind, i, p, n):
                if step == "max":
                    s, r, m, _, _, cols, _ = max_unit(kind, n)
                    dve.wait_ge(max_scored, count(i, p, M_UNITS, n + 1))
                    nc.vector.tensor_reduce(part_max[:, s % 2, r, m:m + 1], max_bank[n % 2][:, 0:cols],
                                            AX.X, ALU.max).then_inc(max_read, 1)
                    if r == 3 and m == s:
                        dve.wait_ge(max_read, count(i, p, M_UNITS, n + 1))
                        nc.vector.tensor_reduce(minus_max[:, s % 2, :], part_max[:, s % 2, :, 0:s + 1],
                                                AX.X, ALU.max, negate=True).then_inc(max_ready, 1)
                elif step == "scores":
                    cols = score_tile(kind, n)[5]
                    if n % 2 == 0:
                        wait_exp(dve, i, p, n)
                        reached(dve, weighed, count(i, p, S_TILES, n - 3))
                        nc.vector.tensor_copy(p_high[:, n % 4, 0:cols],
                                              probs[:, n % 4, 0:cols]).then_inc(high_dve, 1)
                    if n % 4 == 3:
                        wait_high(dve, i, p, n)
                        reached(dve, weighed, count(i, p, S_TILES, n - 3))
                        nc.vector.tensor_tensor(p_low[:, n % 4, 0:cols], probs[:, n % 4, 0:cols],
                                                p_high[:, n % 4, 0:cols].bitcast(F32),
                                                ALU.subtract).then_inc(low_dve, 1)
                elif step == "values":
                    s, at, qb = score_tile(kind, n)[:3]
                    if at == 4 * (s + 1) - 1:
                        dve.wait_ge(acc_copied, count(i, p, STAGES, s + 1))
                        nc.vector.reciprocal(inv[:, :], acc_s[E:P, :]).then_inc(inv_ready, 1)
                        dve.wait_ge(inv_ready, count(i, p, STAGES, s + 1))
                        if s == 0:
                            reached(dve, o_low_ready, count(i, p, 1, 0))
                        rows = slice(qb * NQ // 16, (qb + 1) * NQ // 16)
                        for a in range(2):
                            top = acc_s[0:E, :].rearrange("e (r j a) -> e a j r", j=JP, a=2)[:, a]
                            below_ = inv[:, :].rearrange("e (r j a) -> e a j r", j=JP, a=2)[:, a]
                            last = nc.vector.tensor_tensor(o_full[a * E:(a + 1) * E, :, rows], top, below_,
                                                           ALU.mult)
                        last.then_inc(o_ready, 1)
                elif step == "project" and n % 3 == 2:
                    half = n // 3
                    dve.wait_ge(projected, count(i, p, 2, half - 1))
                    dve.wait_ge(res_loaded, 16 * count(i, p, 1, 0))
                    nc.vector.tensor_tensor(res[:, half, :], side[:, :], res[:, half, :],
                                            ALU.add).then_inc(added, 1)

            heads(dve, do)

        @block.tensor
        def _(pe):
            pe.wait_ge(consts, 4)
            pe.wait_ge(cleared, 10)

            def do(step, kind, i, p, n):
                if step == "max":
                    _, _, _, qc, key, cols, square = max_unit(kind, n)
                    if n == 0:
                        pe.wait_ge(pool_split, count(i, p, RAW_UNITS, RAW_UNITS))
                    reached(pe, max_read, count(i, p, M_UNITS, n - 1))
                    to = max_bank[n % 2]
                    last = nc.tensor.matmul(to[:, 0:cols], q1[:, p, qc * P:(qc + 1) * P],
                                            k1[:, p, key:key + cols], start=True, stop=(square is None))
                    if square is not None:
                        at = square - key
                        last = nc.tensor.matmul(to[:, at:at + P], eye_b[:, :],
                                                (beyond if kind == LB else below)[:, :], start=False, stop=True)
                    last.then_inc(max_scored, 1)
                elif step == "shift":
                    pe.wait_ge(max_ready, count(i, p, STAGES, n + 1))
                    reached(pe, shift_ready, count(i, p, STAGES, n))
                    if n == 3:
                        reached(pe, added, count(i, p, 2, 0))
                    for r in range(4):
                        at = r if kind == LB else 3 - r
                        last = nc.tensor.matmul(side[:, at * P:(at + 1) * P],
                                                minus_max[:, n % 2, r:r + 1].broadcast_to([P, P]),
                                                eye_r[:, :], start=True, stop=True)
                    last.then_inc(row_ready, 1)
                elif step == "scores":
                    s, at, qb, j, col, cols, square = score_tile(kind, n)
                    if at == 0:
                        pe.wait_ge(shift_ready, count(i, p, STAGES, s + 1))
                    if n % 2:
                        reached(pe, high_act, count(i, p, S_TILES // 2, n // 2 - 1))
                    else:
                        reached(pe, exp_done, count(i, p, S_TILES, n - 3))
                    keys = slice(j * P, (j + 1) * P)
                    queries = slice(qb * NQ + col, qb * NQ + col + cols)
                    to = scores[n % 4]
                    nc.tensor.matmul(to[:, 0:cols], k1[:, p, keys], q1[:, p, queries], start=True, stop=False)
                    if square is not None:
                        nc.tensor.matmul(to[:, square - col:square - col + P], eye_b[:, :],
                                         (below if kind == LB else beyond)[:, :], start=False, stop=False)
                    nc.tensor.matmul(to[:, 0:cols], k2[:, p, keys], q2[:, p, queries],
                                     start=False, stop=True).then_inc(scored, 1)
                elif step == "values":
                    s, at, _, j, col, cols, _ = score_tile(kind, n)
                    first, final = at == 0, at == 4 * (s + 1) - 1
                    if first:
                        reached(pe, acc_copied, count(i, p, STAGES, s))
                    wait_low(pe, i, p, n)
                    high, low = p_high[:, n % 4, 0:cols], p_low[:, n % 4, 0:cols]
                    nc.tensor.matmul(acc[:, col:col + cols], v[:, p, j, 0:P], high, start=first, stop=False,
                                     skip_group_check=True)
                    nc.tensor.matmul(acc[0:E + 1, col:col + cols], v[:, p, j, P:VC], high, start=False,
                                     stop=False, skip_group_check=True)
                    nc.tensor.matmul(acc[:, col:col + cols], v[:, p, j, 0:P], low, start=False, stop=final,
                                     skip_group_check=True).then_inc(weighed, 1)
                elif step == "project":
                    half, third = n // 3, n % 3
                    if n == 0:
                        pe.wait_ge(o_low_ready, count(i, p, 1, 0))
                        reached(pe, shift_ready, shifts_before(i, p))
                    elif n == 3:
                        pe.wait_ge(added, count(i, p, 2, -1))
                    cols = slice(half * NQ, (half + 1) * NQ)
                    products = [(j, o, w) for j in range(JP)
                                for o, w in ((o_high, wo_h), (o_high, wo_l), (o_low, wo_h))]
                    for k in range(third * 8, third * 8 + 8):
                        j, o, w = products[k]
                        last = nc.tensor.matmul(side[:, :], o[:, j, :], w[:, j, cols],
                                                start=(k == 0), stop=(k == 23))
                    if third == 2:
                        last.then_inc(projected, 1)

            def shifts_before(i, p):
                if isinstance(i, int) and i == PAIRS:
                    return G_HEADS * STAGES
                return count(i, p, STAGES, 3)

            heads(pe, do)


def build(nc, xT, x_res, wqk, wv, wo, qk_s, v_s, out):
    project(nc, xT, wqk, wv, qk_s, v_s)
    attend(nc, x_res, wo, qk_s, v_s, out)


def kernel(**inputs):
    import numpy as np
    import concourse.bacc as bacc
    from concourse.bass_utils import run_bass_kernel_spmd as run

    def f32(a):
        return np.asarray(a)

    nc = bacc.Bacc("TRN2", target_bir_lowering=False, num_devices=1)
    x = f32(inputs["x"])
    tokens = x.reshape(B, T, D)
    weights = {w: f32(inputs[f"L0_conv_{w}"]) for w in
               ("Wq_lb", "Wk_lb", "Wv_lb", "Wq_la", "Wk_la", "Wv_la", "Wo")}
    qk = np.stack([weights[w].reshape(4, P, NC, P) for w in ("Wq_lb", "Wk_lb", "Wq_la", "Wk_la")])
    v = np.stack([weights[w].reshape(NQ, V_RAWS, 2, P) for w in ("Wv_lb", "Wv_la")])
    arrays = {
        "xT": tokens.transpose(0, 2, 1).reshape(B, NC, P, T),
        "x_res": tokens.reshape(B, KINDS, HEADS, P, D).transpose(1, 0, 2, 3, 4).reshape(G_HEADS, P, D),
        "wqk": qk.transpose(0, 1, 4, 3, 2).reshape(BLOCKS, P, D),
        "wv": v.transpose(0, 2, 4, 3, 1).reshape(KINDS, V_RAWS, P, D),
        "wo": weights["Wo"].reshape(D, JP, P).transpose(2, 1, 0),
    }
    arrays = {k: np.ascontiguousarray(a) for k, a in arrays.items()}
    ins = {k: nc.dram_tensor(k, a.shape, F32, kind="ExternalInput").ap() for k, a in arrays.items()}
    qk_s = nc.dram_tensor("qk_s", (G_HEADS, P, T), F32, kind="Internal").ap()
    v_s = nc.dram_tensor("v_s", (G_HEADS, P, TOK, E), F32, kind="Internal").ap()
    out = nc.dram_tensor("out", (G_HEADS, P, D), F32, kind="ExternalOutput").ap()
    build(nc, ins["xT"], ins["x_res"], ins["wqk"], ins["wv"], ins["wo"], qk_s, v_s, out)
    result = run(nc, [arrays], core_ids=[0])
    rows = result.results[0]["out"].reshape(KINDS, B, HEADS, P, D).transpose(1, 0, 2, 3, 4)
    return rows.reshape(x.shape)
```

```python
from contextlib import ExitStack

import concourse.bass as bass
from concourse import mybir

F32 = mybir.dt.float32
F32R = mybir.dt.float32r
BF16 = mybir.dt.bfloat16
ALU = mybir.AluOpType
ACT = mybir.ActivationFunctionType
AX = mybir.AxisListType

P = 128
B = 2
T = 2048
D = 1024
E = 64
HEADS = 8
KINDS = 2
LB, LA = 0, 1
G_HEADS = KINDS * B * HEADS
NC = D // P
NQ = 512
GROUP = 32
GN_EPS = 1e-5
SCALE = float(E) ** -0.5
MASKED = -1.0e30



def reached(eng, sem, value):
    if isinstance(value, int) and value <= 0:
        return
    eng.wait_ge(sem, value)



BLOCKS = 16
PAIR_BLOCKS = 8
V_RAWS = 4
TOK = T // P
TILES_KIND = PAIR_BLOCKS * (T // NQ) + TOK
RAWS_KIND = PAIR_BLOCKS + V_RAWS
HALF = T // 2
X_UNITS = 2 * NC
X_SLOTS = 4


def project(nc, xT, wqk, wv, qk_s, v_s):
    with ExitStack() as ctx:
        def sb(name, shape, dt=F32):
            return ctx.enter_context(nc.sbuf_tensor(name, shape, dt))

        def sem(name):
            return ctx.enter_context(nc.semaphore(name))

        xh = sb("xh", [P, NC, T], F32R)
        xl = sb("xl", [P, NC, T], F32R)
        xs = sb("xs", [P, X_SLOTS, HALF])
        w_raw = sb("w_raw", [P, D])
        wh = sb("wh", [P, 2, NC, P], F32R)
        wl = sb("wl", [P, 2, NC, P], F32R)
        vh = sb("vh", [P, NC, NQ], F32R)
        vl = sb("vl", [P, NC, NQ], F32R)
        stage_a = sb("stage_a", [P, 2, NQ])
        stage_d = sb("stage_d", [P, 2, NQ])
        average = sb("average", [P, P])
        stats = sb("stats", [P, NC, T // NQ, 6])
        channel = sb("channel", [P, NC, 2])
        centre = sb("centre", [P, NC])
        square = sb("square", [P, NC])
        spread = sb("spread", [P, NC])
        group_mean = sb("group_mean", [P, NC])
        group_var = sb("group_var", [P, NC])
        deviation = sb("deviation", [P, NC])
        inverse = sb("inverse", [P, NC])
        bank = [ctx.enter_context(nc.psum_tensor(f"proj{n}", [P, NQ], F32)) for n in range(8)]

        x_loaded = [sem(f"x_loaded{n}") for n in range(X_SLOTS)]
        w_loaded = sem("w_loaded")
        average_ready = sem("average_ready")
        dve_step = sem("dve_step")
        channel_ready = sem("channel_ready")
        mean_summed = sem("mean_summed")
        spread_ready = sem("spread_ready")
        var_summed = sem("var_summed")
        var_ready = sem("var_ready")
        deviation_ready = sem("deviation_ready")
        x_normal = sem("x_normal")
        x_high = sem("x_high")
        x_low_pool = sem("x_low_pool")
        x_low_dve = sem("x_low_dve")
        x_counted = sem("x_counted")
        w_high = sem("w_high")
        w_low = sem("w_low")
        tile_done = sem("tile_done")
        out_a = sem("out_a")
        out_d = sem("out_d")
        stored_a = [sem(f"stored_a{n}") for n in range(2)]
        stored_d = [sem(f"stored_d{n}") for n in range(2)]

        def blocks(eng, final, body):
            for u in range(2):
                body(u, u, True)
            turns = PAIR_BLOCKS // 2 - final
            with eng.Fori(1, turns) as m:
                for u in range(2):
                    body(2 * m + u, u, True)
            if final:
                for u in range(2):
                    body(2 * turns + u, u, False)

        def tile(b, kind, t):
            return (b * KINDS + kind) * TILES_KIND + t

        def raw(b, kind, r):
            return 2 + (b * KINDS + kind) * RAWS_KIND + r

        def x_unit(b, again, h):
            return (2 * b + again) * X_UNITS + h

        V_TILES = PAIR_BLOCKS * (T // NQ)

        block = ctx.enter_context(nc.Block())

        @block.sync
        def _(sp):
            def load_w(src, r):
                reached(sp, w_low, r)
                sp.dma_start(w_raw[:, :], src).then_inc(w_loaded, 16)

            def load_x(b, again, h):
                n = x_unit(b, again, h)
                k, earlier = n - X_SLOTS, (n - X_SLOTS) // X_UNITS
                if k >= 0 and earlier % 2 == 0:
                    sp.wait_ge(x_counted, earlier // 2 * X_UNITS + k % X_UNITS + 1)
                elif k >= 0:
                    sp.wait_ge((x_low_pool, x_low_dve)[k % 2],
                               earlier // 2 * NC + k % X_UNITS // 2 + 1)
                src = xT[b, h // 2][:, (h % 2) * HALF:(h % 2 + 1) * HALF]
                sp.dma_start(xs[:, n % X_SLOTS, :], src).then_inc(x_loaded[n % X_SLOTS], 16)

            def store(dst, t, n):
                done, stage, stored = ((out_a, stage_a, stored_a), (out_d, stage_d, stored_d))[t % 2]
                slot = (t // 2) % 2
                sp.wait_ge(done, n // 2 + 1)
                sp.dma_start(dst, stage[:, slot, :]).then_inc(stored[slot], 16)

            for h in range(X_SLOTS):
                load_x(0, False, h)
            for n in range(2):
                load_w(wqk[n], n)
            for h in range(X_SLOTS, X_UNITS):
                load_x(0, False, h)
            for b in range(B):
                for h in range(X_UNITS):
                    load_x(b, True, h)
                for kind in range(KINDS):
                    for r in range(V_RAWS):
                        load_w(wv[kind, r], raw(b, kind, r))

                    def one(n, u, more, b=b, kind=kind):
                        if more:
                            later = (n + (kind * PAIR_BLOCKS + 2)) % BLOCKS
                            load_w(wqk[bass.ds(later, 1)].rearrange("a p d -> (a p) d"),
                                   n + raw(b, kind, V_RAWS))
                        row = n // 4 * (B * 4) + n % 4 + (kind * 2 * B + b) * 4
                        for q in range(T // NQ):
                            store(qk_s[bass.ds(row, 1), :, q * NQ:(q + 1) * NQ].rearrange("a p t -> (a p) t"),
                                  4 * u + q, n * 4 + tile(b, kind, q))

                    blocks(sp, b == B - 1 and kind == KINDS - 1, one)
                    for t in range(TOK):
                        heads = v_s[(kind * B + b) * HEADS:(kind * B + b + 1) * HEADS, :, t, :]
                        if b == 0 and kind == 0:
                            load_x(1, False, t)
                        store(heads.rearrange("h p e -> p h e"), t, tile(b, kind, V_TILES + t))
            for s in (*stored_a, *stored_d):
                sp.wait_ge(s, 16 * (B * KINDS * TILES_KIND // 4))

        def low_x(eng, b, h, done):
            slot, cols = x_unit(b, True, h) % X_SLOTS, slice((h % 2) * HALF, (h % 2 + 1) * HALF)
            eng.wait_ge(x_high, b * X_UNITS + h + 1)
            eng.tensor_tensor(xl[:, h // 2, cols], xs[:, slot, :], xh[:, h // 2, cols].bitcast(F32),
                              ALU.subtract).then_inc(done, 1)

        @block.gpsimd
        def _(pool):
            for b in range(B):
                for h in range(0, X_UNITS, 2):
                    low_x(pool, b, h, x_low_pool)

        @block.tensor
        def _(pe):
            products = ((wh, xh), (wh, xl), (wl, xh))
            pe.wait_ge(average_ready, 5)
            for b in range(B):
                reached(pe, out_a, tile(b, 0, 0) // 2)
                reached(pe, out_d, tile(b, 0, 0) // 2)
                pe.wait_ge(channel_ready, b + 1)
                nc.tensor.matmul(bank[6][:, 0:NC], average[:, :], channel[:, :, 0],
                                 start=True, stop=True).then_inc(mean_summed, 1)
                pe.wait_ge(spread_ready, b + 1)
                nc.tensor.matmul(bank[7][:, 0:NC], average[:, :], spread[:, :],
                                 start=True, stop=True).then_inc(var_summed, 1)

                def both_first_blocks(b=b):
                    pe.wait_ge(w_low, raw(b, 0, 0))
                    pe.wait_ge(var_ready, b + 1)
                    for c in range(NC):
                        pe.wait_ge(x_low_pool, b * NC + c + 1)
                        pe.wait_ge(x_low_dve, b * NC + c + 1)
                        for t in range(8):
                            for w, x in products:
                                last = nc.tensor.matmul(
                                    bank[t][:, :], w[:, t // 4, c, :], x[:, c, t % 4 * NQ:(t % 4 + 1) * NQ],
                                    start=(c == 0 and w is wh and x is xh),
                                    stop=(c == NC - 1 and w is wl))
                            if c == NC - 1:
                                last.then_inc(tile_done, 1)

                for kind in range(KINDS):
                    def one(n, u, more, b=b, kind=kind):
                        first = isinstance(n, int) and n < 2
                        if first and kind == 0:
                            if n == 0:
                                both_first_blocks()
                            return
                        pe.wait_ge(w_low, raw(b, kind, n - 1) if first else n + raw(b, kind, V_RAWS - 1))
                        for q in range(T // NQ):
                            reached(pe, (out_a, out_d)[q % 2], n * 2 + (tile(b, kind, q) // 2 - 3))
                            cols = slice(q * NQ, (q + 1) * NQ)
                            for c in range(NC):
                                for w, x in products:
                                    last = nc.tensor.matmul(
                                        bank[4 * u + q][:, :], w[:, u, c, :], x[:, c, cols],
                                        start=(c == 0 and w is wh and x is xh),
                                        stop=(c == NC - 1 and w is wl))
                            last.then_inc(tile_done, 1)

                    blocks(pe, b == B - 1 and kind == KINDS - 1, one)
                    for t in range(TOK):
                        pe.wait_ge((out_a, out_d)[t % 2], tile(b, kind, V_TILES + t) // 2 - 3)
                        cols = slice(t * P, (t + 1) * P)
                        for c in range(NC):
                            for x, w in ((xh, vh), (xh, vl), (xl, vh)):
                                last = nc.tensor.matmul(bank[t % 8][:, :], x[:, c, cols], w[:, c, :],
                                                        start=(c == 0 and x is xh and w is vh),
                                                        stop=(c == NC - 1 and x is xl))
                        last.then_inc(tile_done, 1)

        def split_block(eng, high, u, r, freed):
            reached(eng, tile_done, freed)
            if high:
                eng.wait_ge(w_loaded, r * 16 + 16)
                eng.activation(wh[:, u, :, :], w_raw[:, :].rearrange("p (c e) -> p c e", c=NC),
                               ACT.Copy).then_inc(w_high, 1)
            else:
                eng.wait_ge(w_high, r + 1)
                eng.tensor_tensor(wl[:, u, :, :], w_raw[:, :].rearrange("p (c e) -> p c e", c=NC),
                                  wh[:, u, :, :].bitcast(F32), ALU.subtract).then_inc(w_low, 1)

        def split_v(eng, high, b, kind):
            reached(eng, tile_done, tile(b, kind, 0))
            for k in range(V_RAWS):
                r = raw(b, kind, k)
                cs = slice(2 * k, 2 * k + 2)
                src = w_raw[:, :].rearrange("p (c e) -> p c e", c=2)
                if high:
                    eng.wait_ge(w_loaded, 16 * (r + 1))
                    eng.activation(vh[:, cs, :], src, ACT.Copy).then_inc(w_high, 1)
                else:
                    eng.wait_ge(w_high, r + 1)
                    eng.tensor_tensor(vl[:, cs, :], src, vh[:, cs, :].bitcast(F32),
                                      ALU.subtract).then_inc(w_low, 1)

        def copy_out(eng, t, n, stage, stored, done, copy):
            slot = (t // 2) % 2
            eng.wait_ge(tile_done, n + 1)
            count = n // 4 * 16
            reached(eng, stored[slot], count)
            copy(stage[:, slot, :], bank[t % 8][:, :]).then_inc(done, 1)

        def weights_and_tiles(eng, high, b):
            stage, stored, done = (stage_a, stored_a, out_a) if high else (stage_d, stored_d, out_d)
            copy = eng.copy if high else eng.tensor_copy
            odd = 0 if high else 1
            for kind in range(KINDS):
                split_v(eng, high, b, kind)

                def one(n, u, more, b=b, kind=kind):
                    for q in range(odd, T // NQ, 2):
                        copy_out(eng, 4 * u + q, n * 4 + tile(b, kind, q), stage, stored, done, copy)
                    if more:
                        split_block(eng, high, u, n + raw(b, kind, V_RAWS), n * 4 + tile(b, kind, 4))

                blocks(eng, b == B - 1 and kind == KINDS - 1, one)
                for t in range(odd, TOK, 2):
                    if not high and b == 0 and kind == 0:
                        count_x(1, t - 1)
                        count_x(1, t)
                    copy_out(eng, t, tile(b, kind, V_TILES + t), stage, stored, done, copy)

        def count_x(b, h):
            n = x_unit(b, False, h)
            nc.vector.wait_ge(x_loaded[n % X_SLOTS], 16 * (n // X_SLOTS + 1))
            for q in range(2):
                last = nc.vector.bn_stats(stats[:, h // 2, 2 * (h % 2) + q, :],
                                          xs[:, n % X_SLOTS, q * NQ:(q + 1) * NQ])
            last.then_inc(x_counted, 1)

        @block.scalar
        def _(act):
            for u in range(2):
                split_block(act, True, u, u, 0)
            for b in range(B):
                act.wait_ge(var_ready, b + 1)
                nc.scalar.activation(deviation[:, :], group_var[:, :], ACT.Sqrt).then_inc(deviation_ready, 1)
                for h in range(X_UNITS):
                    n = x_unit(b, True, h)
                    act.wait_ge(x_normal, b * X_UNITS + h + 1)
                    nc.scalar.activation(xh[:, h // 2, (h % 2) * HALF:(h % 2 + 1) * HALF],
                                         xs[:, n % X_SLOTS, :], ACT.Copy).then_inc(x_high, 1)
                weights_and_tiles(act, True, b)

        @block.vector
        def _(dve):
            nc.vector.memset(average[:, :], 0.0).then_inc(average_ready, 1)
            dve.wait_ge(average_ready, 1)
            for k in range(P // GROUP):
                part = slice(k * GROUP, (k + 1) * GROUP)
                nc.vector.memset(average[part, part], 1.0 / GROUP).then_inc(average_ready, 1)

            for u in range(2):
                split_block(dve, False, u, u, 0)
            steps = [0]

            def step(ins):
                steps[0] += 1
                ins.then_inc(dve_step, 1)
                dve.wait_ge(dve_step, steps[0])

            for h in range(X_UNITS):
                count_x(0, h)
            for b in range(B):
                dve.wait_ge(x_counted, (b + 1) * X_UNITS)
                for c in range(NC):
                    last = nc.vector.bn_aggr(channel[:, c, :], stats[:, c, :, :])
                last.then_inc(channel_ready, 1)
                dve.wait_ge(mean_summed, b + 1)
                step(nc.vector.tensor_copy(group_mean[:, :], bank[6][:, 0:NC]))
                step(nc.vector.tensor_tensor(centre[:, :], channel[:, :, 0], group_mean[:, :], ALU.subtract))
                step(nc.vector.tensor_tensor(square[:, :], centre[:, :], centre[:, :], ALU.mult))
                nc.vector.tensor_tensor(spread[:, :], square[:, :], channel[:, :, 1],
                                        ALU.add).then_inc(spread_ready, 1)
                dve.wait_ge(var_summed, b + 1)
                nc.vector.tensor_scalar(group_var[:, :], bank[7][:, 0:NC], GN_EPS, None,
                                        ALU.add).then_inc(var_ready, 1)
                dve.wait_ge(deviation_ready, b + 1)
                step(nc.vector.reciprocal(inverse[:, :], deviation[:, :]))
                reached(dve, tile_done, tile(b, 0, 0))
                for h in range(X_UNITS):
                    n, c = x_unit(b, True, h), h // 2
                    dve.wait_ge(x_loaded[n % X_SLOTS], 16 * (n // X_SLOTS + 1))
                    nc.vector.tensor_scalar(xs[:, n % X_SLOTS, :], xs[:, n % X_SLOTS, :],
                                            group_mean[:, c:c + 1], inverse[:, c:c + 1], ALU.subtract,
                                            ALU.mult).then_inc(x_normal, 1)
                    if h and h % 2 == 0:
                        low_x(dve, b, h - 1, x_low_dve)
                low_x(dve, b, X_UNITS - 1, x_low_dve)
                weights_and_tiles(dve, False, b)



STAGES = T // NQ
S_TILES = 40
M_UNITS = 40
AHEAD = 3
M_AHEAD = 22
PAIRS = G_HEADS // 2
RAW_UNITS = 5
RR = T // 16
JP = 8
OP_PIECES = 6
CR_SLOT = {2: 3, 3: 19, 0: 23, 1: 31}
HIGH_SLOT = {0: 1, 1: 4, 2: 7, 3: 10, 4: 13}
LOW_SLOT = {2 * u + h: at + 1 + h for u, at in HIGH_SLOT.items() for h in range(2)}
DIVIDE_SLOT = {3: 1, 0: 7, 1: 13, 2: 26}
ROUND_SLOT = {"high": 4, "low": 6}
OP_SLOT = {0: 9, 1: 10, 2: 11, 3: 15, 4: 16, 5: 17}
ADD_SLOT = {0: 12, 1: 18}
LOW_DVE = (1, 2)
WO_UNITS = 16
WO_SLOT = {w: 12 + 3 * w // 2 for w in range(WO_UNITS)}
HIGH_DVE = (0,)


def score_tile(kind, t):
    s = 0
    while t >= 4 * (s + 1):
        t -= 4 * (s + 1)
        s += 1
    over = t - 4 * s
    qb, j = (s, t) if kind == LB else (STAGES - 1 - s, TOK - 1 - t)
    if over < 0:
        return s, t, qb, j, 0, NQ, None
    if kind == LB:
        return s, t, qb, j, over * P, NQ - over * P, over * P
    return s, t, qb, j, 0, NQ - over * P, NQ - (over + 1) * P


def max_unit(kind, n):
    s = 0
    while n >= 4 * (s + 1):
        n -= 4 * (s + 1)
        s += 1
    r, m = n // (s + 1), n % (s + 1)
    keys = (4 * s + r + 1) * P
    lo, hi = m * NQ, min(keys, (m + 1) * NQ)
    diagonal = keys - P if hi == keys else None
    if kind == LB:
        return s, r, m, 4 * s + r, lo, hi - lo, diagonal
    return (s, r, m, TOK - 1 - 4 * s - r, T - hi, hi - lo,
            None if diagonal is None else T - keys)


def slots(has_next, has_before):
    plan = []
    for t in range(S_TILES):
        for step, n in (("max", t + M_AHEAD), ("scores", t + AHEAD)):
            if has_next or n < 40:
                plan.append((step, n >= 40, n % 40))
        for s, at in CR_SLOT.items():
            if at == t and (has_next or s >= 2):
                plan.append(("shift", s < 2, s))
        for s, at in DIVIDE_SLOT.items():
            for step, later in (("invert", 0), ("spread", 1), ("divide", 2)):
                if at + later == t and (has_before or s < 3):
                    plan.append((step, False, s))
        for part, at in ROUND_SLOT.items():
            if at == t and has_before:
                plan.append(("round " + part, False, 0))
        for u, at in HIGH_SLOT.items():
            if at == t and has_next:
                plan.append(("split high", True, u))
        for u, at in LOW_SLOT.items():
            if at == t and has_next:
                plan.append(("split low", True, u))
        for n, at in OP_SLOT.items():
            if at == t and has_before:
                plan.append(("project", False, n))
        for half, at in ADD_SLOT.items():
            if at == t and has_before:
                plan.append(("add", False, half))
        for w, at in WO_SLOT.items():
            if at == t and not has_before:
                plan.append(("weights", False, w))
        plan.append(("values", False, t))
    return plan


def prologue():
    return ([(step, False, n) for u in range(RAW_UNITS)
             for step, n in (("split high", u), ("split low", 2 * u), ("split low", 2 * u + 1))]
            + [("max", False, n) for n in range(4)] + [("shift", False, 0)]
            + [("max", False, n) for n in range(4, 12)] + [("shift", False, 1)]
            + [("max", False, n) for n in range(12, M_AHEAD)]
            + [("scores", False, t) for t in range(AHEAD)])


def attend(nc, x_res, wo, qk_s, v_s, out):
    with ExitStack() as ctx:
        def sb(name, shape, dt=F32):
            return ctx.enter_context(nc.sbuf_tensor(name, shape, dt))

        def sem(name):
            return ctx.enter_context(nc.semaphore(name))

        q1 = sb("q1", [P, 2, T], F32R)
        q2 = sb("q2", [P, 2, T], F32R)
        k1 = sb("k1", [P, 2, T], F32R)
        k2 = sb("k2", [P, 2, T], F32R)
        VC = 3 * E + 1
        v = sb("v", [P, 2, TOK, VC], F32R)
        raw = sb("raw", [P, 2, HALF])
        probs = sb("probs", [P, 4, NQ])
        p_high = sb("p_high", [P, 4, NQ], F32R)
        p_low = sb("p_low", [P, 4, NQ], F32R)
        acc_s = sb("acc_s", [P, NQ])
        inv_c = sb("inv_c", [E, NQ // 32])
        inv = sb("inv", [E, NQ])
        o_full = sb("o_full", [P, JP, RR])
        o_high = sb("o_high", [P, JP, RR], F32R)
        o_low = sb("o_low", [P, JP, RR], F32R)
        wo_h = sb("wo_h", [P, JP, D], F32R)
        wo_l = sb("wo_l", [P, JP, D], F32R)
        res = sb("res", [P, 2, NQ])
        part_max = sb("part_max", [P, 2, 4, 4])
        minus_max = sb("minus_max", [P, 2, 4], F32R)
        eye = sb("eye", [P, P])
        eye_r = sb("eye_r", [P, P], F32R)
        eye_b = sb("eye_b", [P, P], BF16)
        below = sb("below", [P, P], BF16)
        beyond = sb("beyond", [P, P], BF16)

        def bank(name):
            return ctx.enter_context(nc.psum_tensor(name, [P, NQ], F32))

        scores = [bank(f"scores{n}") for n in range(2)]
        max_bank = [bank(f"max{n}") for n in range(2)]
        acc = [bank(f"acc{n}") for n in range(2)]
        side = bank("side")
        rows_bank = bank("rows")

        raw_loaded = [sem(f"raw_loaded{n}") for n in range(2)]
        wo_loaded = [sem(f"wo_loaded{n}") for n in range(2)]
        wo_high = sem("wo_high")
        wo_split = sem("wo_split")
        res_loaded = sem("res_loaded")
        cleared = sem("cleared")
        eye_made = sem("eye_made")
        consts = sem("consts")
        act_split = sem("act_split")
        pool_split = sem("pool_split")
        max_scored = sem("max_scored")
        max_read = sem("max_read")
        max_ready = sem("max_ready")
        row_ready = sem("row_ready")
        shift_ready = sem("shift_ready")
        scored = sem("scored")
        exp_done = sem("exp_done")
        high_act = sem("high_act")
        high_dve = sem("high_dve")
        low_pool = sem("low_pool")
        low_dve = sem("low_dve")
        weighed = sem("weighed")
        acc_copied = sem("acc_copied")
        divide_step = sem("divide_step")
        o_ready = sem("o_ready")
        o_high_ready = sem("o_high_ready")
        o_low_ready = sem("o_low_ready")
        projected = sem("projected")
        added = sem("added")
        stored = sem("stored")

        def pairs(eng, body):
            body(0, LB, LB)
            with eng.Fori(1, PAIRS // 2 - 1) as i:
                body(i, LB, LB)
            body(PAIRS // 2 - 1, LB, LA)
            body(PAIRS // 2, LA, LA)
            with eng.Fori(PAIRS // 2 + 1, PAIRS - 1) as i:
                body(i, LA, LA)
            body(PAIRS - 1, LA, None)

        def heads(eng, do):
            for step, _, n in prologue():
                do(step, LB, 0, 0, n)

            def pair(i, kind, then):
                for p in range(2):
                    of = kind if p == 0 else then
                    following = (i, 1) if p == 0 else (i + 1, 0)
                    has_before = p == 1 or not isinstance(i, int) or i > 0
                    for step, later, n in slots(of is not None, has_before):
                        if later:
                            do(step, of, *following, n)
                        else:
                            do(step, kind, i, p, n)

            pairs(eng, pair)
            for step in ("invert", "spread", "divide"):
                do(step, LA, PAIRS, 0, 3)
            for part in ROUND_SLOT:
                do("round " + part, None, PAIRS, 0, 0)
            for half in range(2):
                for n in range(3 * half, 3 * half + 3):
                    do("project", None, PAIRS, 0, n)
                do("add", None, PAIRS, 0, half)

        def count(i, p, per_head, n):
            return i * (2 * per_head) + (p * per_head + n)

        def taken(members, n):
            return n // 4 * len(members) + sum(m <= n % 4 for m in members)

        HIGH_ACT = tuple(m for m in range(4) if m not in HIGH_DVE)

        def wait_one(eng, sem, members, i, p, n):
            reached(eng, sem, count(i, p, S_TILES // 4 * len(members), taken(members, n)))

        def wait_high(eng, i, p, n):
            if n % 4 in HIGH_DVE:
                wait_one(eng, high_dve, HIGH_DVE, i, p, n)
            else:
                wait_one(eng, high_act, HIGH_ACT, i, p, n)

        def wait_low(eng, i, p, n):
            reached(eng, low_dve, count(i, p, S_TILES, n + 1))
            reached(eng, low_pool, count(i, p, S_TILES, n + 1))

        def low_part(eng, done, kind, i, p, n):
            cols = score_tile(kind, n % S_TILES)[5]
            mine = cols * LOW_DVE[0] // LOW_DVE[1]
            part = slice(0, mine) if done is low_dve else slice(mine, cols)
            wait_high(eng, i, p, n)
            reached(eng, weighed, count(i, p, S_TILES, n - 3))
            eng.tensor_tensor(p_low[:, n % 4, part], probs[:, n % 4, part],
                              p_high[:, n % 4, part].bitcast(F32), ALU.subtract).then_inc(done, 1)

        block = ctx.enter_context(nc.Block())

        @block.sync
        def _(sp):
            def load_raw(i, p, kind):
                row = i + kind * PAIRS // 2
                for u in range(RAW_UNITS):
                    slot = (p * RAW_UNITS + u) % 2
                    reached(sp, act_split, count(i, p, 2 * RAW_UNITS, 2 * u - 2))
                    reached(sp, pool_split, count(i, p, 2 * RAW_UNITS, 2 * u - 2))
                    if u < 4:
                        src = qk_s[bass.ds(row + (u // 2) * (B * 4), 1), p * E:(p + 1) * E,
                                   (u % 2) * HALF:(u % 2 + 1) * HALF].rearrange("a e t -> (a e) t")
                        for copy in range(2):
                            sp.dma_start(raw[copy * E:(copy + 1) * E, slot, :], src).then_inc(raw_loaded[slot], 16)
                    else:
                        src = v_s[bass.ds(2 * i + p, 1)].rearrange("a p t e -> (a p) (t e)")
                        for half in range(2):
                            cols = slice(half * NQ, (half + 1) * NQ)
                            sp.dma_start(raw[:, slot, cols], src[:, cols]).then_inc(raw_loaded[slot], 16)

            def residual(g):
                reached(sp, stored, g * 16)
                sp.dma_start(res[:, :, :].rearrange("p a n -> p (a n)"),
                             x_res[bass.ds(g, 1)].rearrange("a p d -> (a p) d")).then_inc(res_loaded, 16)

            def rows_out(g):
                sp.wait_ge(added, g * 2 + 2)
                sp.dma_start(out[bass.ds(g, 1)].rearrange("a p d -> (a p) d"),
                             res[:, :, :].rearrange("p a n -> p (a n)")).then_inc(stored, 16)

            load_raw(0, 0, LB)

            def pair(i, kind, then):
                for p in range(2):
                    of = kind if p == 0 else then
                    if of is not None:
                        load_raw(*((i, 1) if p == 0 else (i + 1, 0)), of)
                    if isinstance(i, int) and i == 0 and p == 0:
                        for w in range(WO_UNITS):
                            reached(sp, wo_split, w - 1)
                            sp.dma_start(res[:, w % 2, :],
                                         wo[:, w // 2, (w % 2) * NQ:(w % 2 + 1) * NQ]).then_inc(wo_loaded[w % 2], 16)
                        sp.wait_ge(wo_split, WO_UNITS)
                        residual(0)
                    if p == 1 or not isinstance(i, int) or i > 0:
                        before = 2 * i + (p - 1)
                        rows_out(before)
                        residual(before + 1)

            pairs(sp, pair)
            rows_out(G_HEADS - 1)
            sp.wait_ge(stored, 16 * G_HEADS)

        @block.gpsimd
        def _(pool):
            nc.gpsimd.memset(eye[:, :], 0.0).then_inc(eye_made, 1)
            nc.gpsimd.memset(below[:, :], 0.0).then_inc(eye_made, 1)
            nc.gpsimd.memset(beyond[:, :], 0.0).then_inc(eye_made, 1)
            pool.wait_ge(eye_made, 3)
            nc.gpsimd.affine_select(out=eye[:, :], in_=eye[:, :], compare_op=ALU.not_equal, fill=1.0,
                                    base=0, pattern=[[-1, P]], channel_multiplier=1).then_inc(eye_made, 1)
            nc.gpsimd.affine_select(out=below[:, :], in_=below[:, :], compare_op=ALU.is_ge, fill=MASKED,
                                    base=0, pattern=[[1, P]], channel_multiplier=-1).then_inc(consts, 1)
            nc.gpsimd.affine_select(out=beyond[:, :], in_=beyond[:, :], compare_op=ALU.is_ge, fill=MASKED,
                                    base=0, pattern=[[-1, P]], channel_multiplier=1).then_inc(consts, 1)

            def do(step, kind, i, p, n):
                if step == "split low":
                    u, h = n // 2, n % 2
                    slot = (p * RAW_UNITS + u) % 2
                    pool.wait_ge(act_split, count(i, p, 2 * RAW_UNITS, 2 * u + 2))
                    reached(pool, pool_split, count(i, p, 2 * RAW_UNITS, n))
                    reached(pool, low_pool, count(i, p, S_TILES, LOW_SLOT[n] + AHEAD - S_TILES + 1))
                    src = slice(h * NQ, (h + 1) * NQ)
                    cols = slice((u % 2) * HALF + h * NQ, (u % 2) * HALF + (h + 1) * NQ)
                    if u < 2:
                        ins = nc.gpsimd.tensor_tensor(q2[0:E, p, cols], raw[0:E, slot, src],
                                                      q1[0:E, p, cols].bitcast(F32), ALU.subtract)
                    elif u < 4:
                        low = k1[E:P, p, cols]
                        ins = nc.gpsimd.tensor_tensor(low, raw[E:P, slot, src], low.bitcast(F32), ALU.subtract)
                    else:
                        js = slice(h * TOK // 2, (h + 1) * TOK // 2)
                        ins = nc.gpsimd.tensor_tensor(
                            v[:, p, js, 2 * E:3 * E], raw[:, slot, src].rearrange("p (t e) -> p t e", e=E),
                            v[:, p, js, 0:E].bitcast(F32), ALU.subtract)
                    ins.then_inc(pool_split, 1)
                    pool.wait_ge(pool_split, count(i, p, 2 * RAW_UNITS, n + 1))
                elif step == "scores":
                    low_part(pool, low_pool, kind, i, p, n)

            heads(pool, do)

        @block.scalar
        def _(act):
            def do(step, kind, i, p, n):
                if step == "split high":
                    slot = (p * RAW_UNITS + n) % 2
                    act.wait_ge(raw_loaded[slot], 32 * (i * RAW_UNITS + ((p * RAW_UNITS + n) // 2 + 1)))
                    reached(act, weighed, count(i, p, S_TILES, -S_TILES))
                    cols = slice((n % 2) * HALF, (n % 2 + 1) * HALF)
                    if n < 2:
                        ins = nc.scalar.activation(q1[:, p, cols], raw[:, slot, :], ACT.Copy)
                    elif n < 4:
                        nc.scalar.activation(k2[0:E, p, cols], raw[0:E, slot, :], ACT.Copy)
                        ins = nc.scalar.activation(k1[:, p, cols], raw[:, slot, :], ACT.Copy)
                    else:
                        ins = nc.scalar.activation(v[:, p, :, 0:E],
                                                   raw[:, slot, :].rearrange("p (t e) -> p t e", e=E), ACT.Copy)
                    ins.then_inc(act_split, 2)
                elif step == "shift":
                    act.wait_ge(row_ready, count(i, p, STAGES, n + 1))
                    qb = n if kind == LB else STAGES - 1 - n
                    nc.scalar.activation(q2[E:E + 1, p, qb * NQ:(qb + 1) * NQ], side[E:E + 1, :],
                                         ACT.Copy).then_inc(shift_ready, 1)
                elif step == "scores":
                    cols = score_tile(kind, n)[5]
                    act.wait_ge(scored, count(i, p, S_TILES, n + 1))
                    wait_low(act, i, p, n - 4)
                    nc.scalar.activation(probs[:, n % 4, 0:cols], scores[n % 2][:, 0:cols], ACT.Exp,
                                         scale=SCALE).then_inc(exp_done, 1)
                    if n % 4 in HIGH_ACT:
                        reached(act, weighed, count(i, p, S_TILES, n - 3))
                        nc.scalar.activation(p_high[:, n % 4, 0:cols], scores[n % 2][:, 0:cols], ACT.Exp,
                                             scale=SCALE).then_inc(high_act, 1)
                elif step == "values":
                    s, at = score_tile(kind, n)[:2]
                    if at == 4 * (s + 1) - 1:
                        act.wait_ge(weighed, count(i, p, S_TILES, n + 1))
                        reached(act, o_ready, count(i, p, STAGES, s))
                        nc.scalar.activation(acc_s[:, :], acc[s % 2][:, :], ACT.Copy).then_inc(acc_copied, 1)
                elif step == "weights":
                    act.wait_ge(wo_loaded[n % 2], 16 * (n // 2 + 1))
                    nc.scalar.activation(wo_h[:, n // 2, (n % 2) * NQ:(n % 2 + 1) * NQ], res[:, n % 2, :],
                                         ACT.Copy).then_inc(wo_high, 1)
                elif step == "round high":
                    act.wait_ge(o_ready, count(i, p, STAGES, 0))
                    reached(act, projected, count(i, p, 2, -2))
                    nc.scalar.activation(o_high[:, :, :], o_full[:, :, :], ACT.Copy).then_inc(o_high_ready, 1)

            heads(act, do)

        @block.vector
        def _(dve):
            for p in range(2):
                nc.vector.memset(q2[E:P, p, :].bitcast(F32), 0.0).then_inc(cleared, 1)
                nc.vector.memset(k2[E:P, p, :].bitcast(F32), 0.0).then_inc(cleared, 1)
                nc.vector.memset(v[:, p, :, E:2 * E].bitcast(F32), 1.0).then_inc(cleared, 1)
                nc.vector.memset(v[:, p, :, 3 * E:VC].bitcast(F32), 0.0).then_inc(cleared, 1)
            dve.wait_ge(cleared, 8)
            for p in range(2):
                nc.vector.memset(k2[E:E + 1, p, :].bitcast(F32), 1.0).then_inc(cleared, 1)
            dve.wait_ge(eye_made, 4)
            nc.vector.tensor_copy(eye_r[:, :], eye[:, :]).then_inc(consts, 1)
            nc.vector.tensor_copy(eye_b[:, :], eye[:, :]).then_inc(consts, 1)
            def divided(i, p, n):
                return count(i, p, 3 * STAGES, 3 * n) if n < 3 else count(i, p, 3 * STAGES, -3)

            def div_kind(kind, i, p, n):
                if n == 3 and p == 0 and isinstance(i, int) and i == PAIRS // 2:
                    return LB
                return kind

            def both_parts(kind, i, p, n):
                if n % 4 in HIGH_DVE:
                    cols = score_tile(kind, n % S_TILES)[5]
                    dve.wait_ge(exp_done, count(i, p, S_TILES, n + 1))
                    reached(dve, weighed, count(i, p, S_TILES, n - 3))
                    nc.vector.tensor_copy(p_high[:, n % 4, 0:cols],
                                          probs[:, n % 4, 0:cols]).then_inc(high_dve, 1)
                low_part(dve, low_dve, kind, i, p, n)

            def do(step, kind, i, p, n):
                if step == "max":
                    s, r, m, _, _, cols, _ = max_unit(kind, n)
                    dve.wait_ge(max_scored, count(i, p, M_UNITS, n + 1))
                    nc.vector.tensor_reduce(part_max[:, s % 2, r, m:m + 1], max_bank[n % 2][:, 0:cols],
                                            AX.X, ALU.max).then_inc(max_read, 1)
                    if r == 3 and m == s:
                        dve.wait_ge(max_read, count(i, p, M_UNITS, n + 1))
                        nc.vector.tensor_reduce(minus_max[:, s % 2, :], part_max[:, s % 2, :, 0:s + 1],
                                                AX.X, ALU.max, negate=True).then_inc(max_ready, 1)
                elif step == "scores":
                    if n or p or not isinstance(i, int) or i:
                        both_parts(kind, i, p, n - 1)
                elif step == "values" and n == S_TILES - 1 - AHEAD:
                    if isinstance(i, int) and (i, p) == (PAIRS - 1, 1):
                        both_parts(kind, i, p, S_TILES - 1)
                elif step == "weights":
                    part = (slice(None), n // 2, slice((n % 2) * NQ, (n % 2 + 1) * NQ))
                    dve.wait_ge(wo_high, n + 1)
                    nc.vector.tensor_tensor(wo_l[part], res[:, n % 2, :], wo_h[part].bitcast(F32),
                                            ALU.subtract).then_inc(wo_split, 1)
                elif step == "invert":
                    done = count(i, p, STAGES, n + 1) if n < 3 else count(i, p, STAGES, 0)
                    steps = divided(i, p, n)
                    dve.wait_ge(acc_copied, done)
                    nc.vector.transpose(inv[:, :], acc_s[E:P, :]).then_inc(divide_step, 1)
                    dve.wait_ge(divide_step, steps + 1)
                    nc.vector.reciprocal(inv_c[:, :], inv[:, :].rearrange("e (b c) -> e b c", c=32)[:, :, 0]
                                         ).then_inc(divide_step, 1)
                elif step == "spread":
                    steps = divided(i, p, n)
                    dve.wait_ge(divide_step, steps + 2)
                    nc.vector.transpose(inv[:, :], inv_c[:, :].rearrange("e (b c) -> e b c", c=1)
                                        .broadcast_to([E, NQ // 32, 32])).then_inc(divide_step, 1)
                elif step == "divide":
                    dve.wait_ge(divide_step, divided(i, p, n) + 3)
                    if n == 0:
                        reached(dve, o_low_ready, count(i, p, 1, 0))
                    qb = n if div_kind(kind, i, p, n) == LB else STAGES - 1 - n
                    rows = slice(qb * NQ // 16, (qb + 1) * NQ // 16)
                    for a in range(2):
                        sums, by = (x.rearrange("e (r j a) -> e a j r", j=JP, a=2)[:, a]
                                    for x in (acc_s[0:E, :], inv[:, :]))
                        last = nc.vector.tensor_tensor(o_full[a * E:(a + 1) * E, :, rows], sums, by, ALU.mult)
                    last.then_inc(o_ready, 1)
                elif step == "round low":
                    dve.wait_ge(o_high_ready, count(i, p, 1, 0))
                    nc.vector.tensor_tensor(o_low[:, :, :], o_full[:, :, :], o_high[:, :, :].bitcast(F32),
                                            ALU.subtract).then_inc(o_low_ready, 1)
                elif step == "add":
                    half = n
                    dve.wait_ge(projected, count(i, p, 2, half - 1))
                    dve.wait_ge(res_loaded, 16 * count(i, p, 1, 0))
                    nc.vector.tensor_tensor(res[:, half, :], rows_bank[:, :], res[:, half, :],
                                            ALU.add).then_inc(added, 1)

            heads(dve, do)

        @block.tensor
        def _(pe):
            pe.wait_ge(consts, 4)
            pe.wait_ge(cleared, 10)

            def do(step, kind, i, p, n):
                if step == "max":
                    _, _, _, qc, key, cols, square = max_unit(kind, n)
                    if n == 0:
                        pe.wait_ge(pool_split, count(i, p, 2 * RAW_UNITS, 2 * RAW_UNITS))
                    reached(pe, max_read, count(i, p, M_UNITS, n - 1))
                    to = max_bank[n % 2]
                    last = nc.tensor.matmul(to[:, 0:cols], q1[:, p, qc * P:(qc + 1) * P],
                                            k1[:, p, key:key + cols], start=True, stop=(square is None))
                    if square is not None:
                        at = square - key
                        last = nc.tensor.matmul(to[:, at:at + P], eye_b[:, :],
                                                (beyond if kind == LB else below)[:, :], start=False, stop=True)
                    last.then_inc(max_scored, 1)
                elif step == "shift":
                    pe.wait_ge(max_ready, count(i, p, STAGES, n + 1))
                    reached(pe, shift_ready, count(i, p, STAGES, n))
                    for r in range(4):
                        at = r if kind == LB else 3 - r
                        last = nc.tensor.matmul(side[:, at * P:(at + 1) * P],
                                                minus_max[:, n % 2, r:r + 1].broadcast_to([P, P]),
                                                eye_r[:, :], start=True, stop=True)
                    last.then_inc(row_ready, 1)
                elif step == "scores":
                    s, at, qb, j, col, cols, square = score_tile(kind, n)
                    if at == 0:
                        pe.wait_ge(shift_ready, count(i, p, STAGES, s + 1))
                    if (n - 2) % 4 in HIGH_ACT:
                        wait_one(pe, high_act, HIGH_ACT, i, p, n - 2)
                    else:
                        reached(pe, exp_done, count(i, p, S_TILES, n - 1))
                    keys = slice(j * P, (j + 1) * P)
                    queries = slice(qb * NQ + col, qb * NQ + col + cols)
                    to = scores[n % 2]
                    nc.tensor.matmul(to[:, 0:cols], k1[:, p, keys], q1[:, p, queries], start=True, stop=False)
                    if square is not None:
                        nc.tensor.matmul(to[:, square - col:square - col + P], eye_b[:, :],
                                         (below if kind == LB else beyond)[:, :], start=False, stop=False)
                    nc.tensor.matmul(to[:, 0:cols], k2[:, p, keys], q2[:, p, queries],
                                     start=False, stop=True).then_inc(scored, 1)
                elif step == "values":
                    s, at, _, j, col, cols, _ = score_tile(kind, n)
                    first, final = at == 0, at == 4 * (s + 1) - 1
                    if first:
                        reached(pe, acc_copied, count(i, p, STAGES, s - 1))
                    wait_low(pe, i, p, n)
                    high, low = p_high[:, n % 4, 0:cols], p_low[:, n % 4, 0:cols]
                    sums = acc[s % 2]
                    nc.tensor.matmul(sums[:, col:col + cols], v[:, p, j, 0:P], high, start=first, stop=False,
                                     skip_group_check=True)
                    nc.tensor.matmul(sums[0:E + 1, col:col + cols], v[:, p, j, P:VC], high, start=False,
                                     stop=False, skip_group_check=True)
                    nc.tensor.matmul(sums[:, col:col + cols], v[:, p, j, 0:P], low, start=False, stop=final,
                                     skip_group_check=True).then_inc(weighed, 1)
                elif step == "project":
                    half, third = n // 3, n % 3
                    if n == 0:
                        pe.wait_ge(o_low_ready, count(i, p, 1, 0))
                    if third == 0:
                        reached(pe, added, count(i, p, 2, half - 2))
                    cols = slice(half * NQ, (half + 1) * NQ)
                    products = [(j, o, w) for j in range(JP)
                                for o, w in ((o_high, wo_h), (o_high, wo_l), (o_low, wo_h))]
                    for k in range(third * 8, third * 8 + 8):
                        j, o, w = products[k]
                        last = nc.tensor.matmul(rows_bank[:, :], o[:, j, :], w[:, j, cols],
                                                start=(k == 0), stop=(k == 23))
                    if third == 2:
                        last.then_inc(projected, 1)

            heads(pe, do)


def build(nc, xT, x_res, wqk, wv, wo, qk_s, v_s, out):
    project(nc, xT, wqk, wv, qk_s, v_s)
    attend(nc, x_res, wo, qk_s, v_s, out)


def kernel(**inputs):
    import numpy as np
    import concourse.bacc as bacc
    from concourse.bass_utils import run_bass_kernel_spmd as run

    def f32(a):
        return np.asarray(a)

    nc = bacc.Bacc("TRN2", target_bir_lowering=False, num_devices=1)
    x = f32(inputs["x"])
    tokens = x.reshape(B, T, D)
    weights = {w: f32(inputs[f"L0_conv_{w}"]) for w in
               ("Wq_lb", "Wk_lb", "Wv_lb", "Wq_la", "Wk_la", "Wv_la", "Wo")}
    qk = np.stack([weights[w].reshape(4, P, NC, P) for w in ("Wq_lb", "Wk_lb", "Wq_la", "Wk_la")])
    v = np.stack([weights[w].reshape(NQ, V_RAWS, 2, P) for w in ("Wv_lb", "Wv_la")])
    arrays = {
        "xT": tokens.transpose(0, 2, 1).reshape(B, NC, P, T),
        "x_res": tokens.reshape(B, KINDS, HEADS, P, D).transpose(1, 0, 2, 3, 4).reshape(G_HEADS, P, D),
        "wqk": qk.transpose(0, 1, 4, 3, 2).reshape(BLOCKS, P, D),
        "wv": v.transpose(0, 2, 4, 3, 1).reshape(KINDS, V_RAWS, P, D),
        "wo": weights["Wo"].reshape(D, JP, P).transpose(2, 1, 0),
    }
    arrays = {k: np.ascontiguousarray(a) for k, a in arrays.items()}
    ins = {k: nc.dram_tensor(k, a.shape, F32, kind="ExternalInput").ap() for k, a in arrays.items()}
    qk_s = nc.dram_tensor("qk_s", (G_HEADS, P, T), F32, kind="Internal").ap()
    v_s = nc.dram_tensor("v_s", (G_HEADS, P, TOK, E), F32, kind="Internal").ap()
    out = nc.dram_tensor("out", (G_HEADS, P, D), F32, kind="ExternalOutput").ap()
    build(nc, ins["xT"], ins["x_res"], ins["wqk"], ins["wv"], ins["wo"], qk_s, v_s, out)
    result = run(nc, [arrays], core_ids=[0])
    rows = result.results[0]["out"].reshape(KINDS, B, HEADS, P, D).transpose(1, 0, 2, 3, 4)
    return rows.reshape(x.shape)
```

```python
from contextlib import ExitStack

import concourse.bass as bass
from concourse import mybir

F32 = mybir.dt.float32
F32R = mybir.dt.float32r
BF16 = mybir.dt.bfloat16
ALU = mybir.AluOpType
ACT = mybir.ActivationFunctionType
AX = mybir.AxisListType

P = 128
B = 2
T = 2048
D = 1024
E = 64
HEADS = 8
KINDS = 2
LB, LA = 0, 1
G_HEADS = KINDS * B * HEADS
NC = D // P
NQ = 512
GROUP = 32
GN_EPS = 1e-5
SCALE = float(E) ** -0.5
MASKED = -1.0e30



def reached(eng, sem, value):
    if isinstance(value, int) and value <= 0:
        return
    eng.wait_ge(sem, value)



BLOCKS = 16
PAIR_BLOCKS = 8
V_RAWS = 4
TOK = T // P
TILES_KIND = PAIR_BLOCKS * (T // NQ) + TOK
RAWS_KIND = PAIR_BLOCKS + V_RAWS
HALF = T // 2
X_UNITS = 2 * NC
X_SLOTS = 4
FIRST_BEHIND = (7, 12)
V_BEHIND = (4, 7, 10, 13)


def project(nc, xT, wqk, wv, qk_s, v_s):
    with ExitStack() as ctx:
        def sb(name, shape, dt=F32):
            return ctx.enter_context(nc.sbuf_tensor(name, shape, dt))

        def sem(name):
            return ctx.enter_context(nc.semaphore(name))

        xh = sb("xh", [P, NC, T], F32R)
        xl = sb("xl", [P, NC, T], F32R)
        xs = sb("xs", [P, X_SLOTS, HALF])
        w_raw = sb("w_raw", [P, D])
        wh = sb("wh", [P, 2, NC, P], F32R)
        wl = sb("wl", [P, 2, NC, P], F32R)
        vh = sb("vh", [P, NC, NQ], F32R)
        vl = sb("vl", [P, NC, NQ], F32R)
        stage_a = sb("stage_a", [P, 2, NQ])
        stage_d = sb("stage_d", [P, 2, NQ])
        average = sb("average", [P, P])
        stats = sb("stats", [P, NC, T // NQ, 6])
        channel = sb("channel", [P, NC, 2])
        centre = sb("centre", [P, NC])
        square = sb("square", [P, NC])
        spread = sb("spread", [P, NC])
        group_mean = sb("group_mean", [P, NC])
        group_var = sb("group_var", [P, NC])
        deviation = sb("deviation", [P, NC])
        inverse = sb("inverse", [P, NC])
        bank = [ctx.enter_context(nc.psum_tensor(f"proj{n}", [P, NQ], F32)) for n in range(8)]

        x_loaded = [sem(f"x_loaded{n}") for n in range(X_SLOTS)]
        w_loaded = sem("w_loaded")
        average_ready = sem("average_ready")
        dve_step = sem("dve_step")
        channel_ready = sem("channel_ready")
        mean_summed = sem("mean_summed")
        spread_ready = sem("spread_ready")
        var_summed = sem("var_summed")
        var_ready = sem("var_ready")
        deviation_ready = sem("deviation_ready")
        x_normal = sem("x_normal")
        x_high = sem("x_high")
        x_low_pool = sem("x_low_pool")
        x_low_dve = sem("x_low_dve")
        x_counted = sem("x_counted")
        w_high = sem("w_high")
        w_low = sem("w_low")
        tile_done = sem("tile_done")
        out_a = sem("out_a")
        out_d = sem("out_d")
        stored_a = [sem(f"stored_a{n}") for n in range(2)]
        stored_d = [sem(f"stored_d{n}") for n in range(2)]

        def blocks(eng, final, body):
            for u in range(2):
                body(u, u, True)
            turns = PAIR_BLOCKS // 2 - final
            with eng.Fori(1, turns) as m:
                for u in range(2):
                    body(2 * m + u, u, True)
            if final:
                for u in range(2):
                    body(2 * turns + u, u, False)

        def tile(b, kind, t):
            return (b * KINDS + kind) * TILES_KIND + t

        def raw(b, kind, r):
            return 2 + (b * KINDS + kind) * RAWS_KIND + r

        def x_unit(b, again, h):
            return (2 * b + again) * X_UNITS + h

        V_TILES = PAIR_BLOCKS * (T // NQ)

        block = ctx.enter_context(nc.Block())

        @block.sync
        def _(sp):
            def load_w(src, r):
                reached(sp, w_low, r)
                sp.dma_start(w_raw[:, :], src).then_inc(w_loaded, 16)

            def load_x(b, again, h):
                n = x_unit(b, again, h)
                k, earlier = n - X_SLOTS, (n - X_SLOTS) // X_UNITS
                if k >= 0 and earlier % 2 == 0:
                    sp.wait_ge(x_counted, earlier // 2 * X_UNITS + k % X_UNITS + 1)
                elif k >= 0:
                    sp.wait_ge((x_low_pool, x_low_dve)[k % 2],
                               earlier // 2 * NC + k % X_UNITS // 2 + 1)
                src = xT[b, h // 2][:, (h % 2) * HALF:(h % 2 + 1) * HALF]
                sp.dma_start(xs[:, n % X_SLOTS, :], src).then_inc(x_loaded[n % X_SLOTS], 16)

            def store(dst, t, n):
                done, stage, stored = ((out_a, stage_a, stored_a), (out_d, stage_d, stored_d))[t % 2]
                slot = (t // 2) % 2
                sp.wait_ge(done, n // 2 + 1)
                sp.dma_start(dst, stage[:, slot, :]).then_inc(stored[slot], 16)

            for h in range(X_UNITS):
                load_x(0, False, h)
                if h in FIRST_BEHIND:
                    n = FIRST_BEHIND.index(h)
                    load_w(wqk[n], n)
            for b in range(B):
                for h in range(X_UNITS):
                    load_x(b, True, h)
                    if h in V_BEHIND:
                        k = V_BEHIND.index(h)
                        load_w(wv[LB, k], raw(b, LB, k))
                for kind in range(KINDS):
                    if kind == LA:
                        for k in range(V_RAWS):
                            load_w(wv[kind, k], raw(b, kind, k))

                    def one(n, u, more, b=b, kind=kind):
                        if more:
                            later = (n + (kind * PAIR_BLOCKS + 2)) % BLOCKS
                            load_w(wqk[bass.ds(later, 1)].rearrange("a p d -> (a p) d"),
                                   n + raw(b, kind, V_RAWS))
                        row = n // 4 * (B * 4) + n % 4 + (kind * 2 * B + b) * 4
                        for q in range(T // NQ):
                            store(qk_s[bass.ds(row, 1), :, q * NQ:(q + 1) * NQ].rearrange("a p t -> (a p) t"),
                                  4 * u + q, n * 4 + tile(b, kind, q))

                    blocks(sp, b == B - 1 and kind == KINDS - 1, one)
                    for t in range(TOK):
                        heads = v_s[(kind * B + b) * HEADS:(kind * B + b + 1) * HEADS, :, t, :]
                        if b == 0 and kind == 0:
                            load_x(1, False, t)
                        store(heads.rearrange("h p e -> p h e"), t, tile(b, kind, V_TILES + t))
            for s in (*stored_a, *stored_d):
                sp.wait_ge(s, 16 * (B * KINDS * TILES_KIND // 4))

        def low_x(eng, b, h, done):
            slot, cols = x_unit(b, True, h) % X_SLOTS, slice((h % 2) * HALF, (h % 2 + 1) * HALF)
            eng.wait_ge(x_high, b * X_UNITS + h + 1)
            eng.tensor_tensor(xl[:, h // 2, cols], xs[:, slot, :], xh[:, h // 2, cols].bitcast(F32),
                              ALU.subtract).then_inc(done, 1)

        @block.gpsimd
        def _(pool):
            for b in range(B):
                for h in range(0, X_UNITS, 2):
                    low_x(pool, b, h, x_low_pool)

        @block.tensor
        def _(pe):
            products = ((wh, xh), (wh, xl), (wl, xh))
            pe.wait_ge(average_ready, 5)
            for b in range(B):
                reached(pe, out_a, tile(b, 0, 0) // 2)
                reached(pe, out_d, tile(b, 0, 0) // 2)
                pe.wait_ge(channel_ready, b + 1)
                nc.tensor.matmul(bank[6][:, 0:NC], average[:, :], channel[:, :, 0],
                                 start=True, stop=True).then_inc(mean_summed, 1)
                pe.wait_ge(spread_ready, b + 1)
                nc.tensor.matmul(bank[7][:, 0:NC], average[:, :], spread[:, :],
                                 start=True, stop=True).then_inc(var_summed, 1)

                def both_first_blocks(b=b):
                    pe.wait_ge(w_low, raw(b, 0, 0))
                    pe.wait_ge(var_ready, b + 1)
                    for c in range(NC):
                        pe.wait_ge(x_low_pool, b * NC + c + 1)
                        pe.wait_ge(x_low_dve, b * NC + c + 1)
                        for t in range(8):
                            for w, x in products:
                                last = nc.tensor.matmul(
                                    bank[t][:, :], w[:, t // 4, c, :], x[:, c, t % 4 * NQ:(t % 4 + 1) * NQ],
                                    start=(c == 0 and w is wh and x is xh),
                                    stop=(c == NC - 1 and w is wl))
                            if c == NC - 1:
                                last.then_inc(tile_done, 1)

                for kind in range(KINDS):
                    def one(n, u, more, b=b, kind=kind):
                        first = isinstance(n, int) and n < 2
                        if first and kind == 0:
                            if n == 0:
                                both_first_blocks()
                            return
                        pe.wait_ge(w_low, raw(b, kind, n - 1) if first else n + raw(b, kind, V_RAWS - 1))
                        for q in range(T // NQ):
                            reached(pe, (out_a, out_d)[q % 2], n * 2 + (tile(b, kind, q) // 2 - 3))
                            cols = slice(q * NQ, (q + 1) * NQ)
                            for c in range(NC):
                                for w, x in products:
                                    last = nc.tensor.matmul(
                                        bank[4 * u + q][:, :], w[:, u, c, :], x[:, c, cols],
                                        start=(c == 0 and w is wh and x is xh),
                                        stop=(c == NC - 1 and w is wl))
                            last.then_inc(tile_done, 1)

                    blocks(pe, b == B - 1 and kind == KINDS - 1, one)
                    for t in range(TOK):
                        pe.wait_ge((out_a, out_d)[t % 2], tile(b, kind, V_TILES + t) // 2 - 3)
                        cols = slice(t * P, (t + 1) * P)
                        for c in range(NC):
                            for x, w in ((xh, vh), (xh, vl), (xl, vh)):
                                last = nc.tensor.matmul(bank[t % 8][:, :], x[:, c, cols], w[:, c, :],
                                                        start=(c == 0 and x is xh and w is vh),
                                                        stop=(c == NC - 1 and x is xl))
                        last.then_inc(tile_done, 1)

        def split_block(eng, high, u, r, freed):
            reached(eng, tile_done, freed)
            if high:
                eng.wait_ge(w_loaded, r * 16 + 16)
                eng.activation(wh[:, u, :, :], w_raw[:, :].rearrange("p (c e) -> p c e", c=NC),
                               ACT.Copy).then_inc(w_high, 1)
            else:
                eng.wait_ge(w_high, r + 1)
                eng.tensor_tensor(wl[:, u, :, :], w_raw[:, :].rearrange("p (c e) -> p c e", c=NC),
                                  wh[:, u, :, :].bitcast(F32), ALU.subtract).then_inc(w_low, 1)

        def split_v(eng, high, b, kind, parts=range(V_RAWS)):
            reached(eng, tile_done, tile(b, kind, 0))
            for k in parts:
                r = raw(b, kind, k)
                cs = slice(2 * k, 2 * k + 2)
                src = w_raw[:, :].rearrange("p (c e) -> p c e", c=2)
                if high:
                    eng.wait_ge(w_loaded, 16 * (r + 1))
                    eng.activation(vh[:, cs, :], src, ACT.Copy).then_inc(w_high, 1)
                else:
                    eng.wait_ge(w_high, r + 1)
                    eng.tensor_tensor(vl[:, cs, :], src, vh[:, cs, :].bitcast(F32),
                                      ALU.subtract).then_inc(w_low, 1)

        def copy_out(eng, t, n, stage, stored, done, copy):
            slot = (t // 2) % 2
            eng.wait_ge(tile_done, n + 1)
            count = n // 4 * 16
            reached(eng, stored[slot], count)
            copy(stage[:, slot, :], bank[t % 8][:, :]).then_inc(done, 1)

        def weights_and_tiles(eng, high, b):
            stage, stored, done = (stage_a, stored_a, out_a) if high else (stage_d, stored_d, out_d)
            copy = eng.copy if high else eng.tensor_copy
            odd = 0 if high else 1
            for kind in range(KINDS):
                if kind == LA:
                    split_v(eng, high, b, kind)

                def one(n, u, more, b=b, kind=kind):
                    for q in range(odd, T // NQ, 2):
                        copy_out(eng, 4 * u + q, n * 4 + tile(b, kind, q), stage, stored, done, copy)
                    if more:
                        split_block(eng, high, u, n + raw(b, kind, V_RAWS), n * 4 + tile(b, kind, 4))

                blocks(eng, b == B - 1 and kind == KINDS - 1, one)
                for t in range(odd, TOK, 2):
                    if not high and b == 0 and kind == 0:
                        count_x(1, t - 1)
                        count_x(1, t)
                    copy_out(eng, t, tile(b, kind, V_TILES + t), stage, stored, done, copy)

        def count_x(b, h):
            n = x_unit(b, False, h)
            nc.vector.wait_ge(x_loaded[n % X_SLOTS], 16 * (n // X_SLOTS + 1))
            for q in range(2):
                last = nc.vector.bn_stats(stats[:, h // 2, 2 * (h % 2) + q, :],
                                          xs[:, n % X_SLOTS, q * NQ:(q + 1) * NQ])
            last.then_inc(x_counted, 1)

        @block.scalar
        def _(act):
            for u in range(2):
                split_block(act, True, u, u, 0)
            for b in range(B):
                act.wait_ge(var_ready, b + 1)
                nc.scalar.activation(deviation[:, :], group_var[:, :], ACT.Sqrt).then_inc(deviation_ready, 1)
                for h in range(X_UNITS):
                    n = x_unit(b, True, h)
                    act.wait_ge(x_normal, b * X_UNITS + h + 1)
                    nc.scalar.activation(xh[:, h // 2, (h % 2) * HALF:(h % 2 + 1) * HALF],
                                         xs[:, n % X_SLOTS, :], ACT.Copy).then_inc(x_high, 1)
                    if h - 1 in V_BEHIND:
                        split_v(act, True, b, LB, (V_BEHIND.index(h - 1),))
                weights_and_tiles(act, True, b)

        @block.vector
        def _(dve):
            nc.vector.memset(average[:, :], 0.0).then_inc(average_ready, 1)
            dve.wait_ge(average_ready, 1)
            for k in range(P // GROUP):
                part = slice(k * GROUP, (k + 1) * GROUP)
                nc.vector.memset(average[part, part], 1.0 / GROUP).then_inc(average_ready, 1)

            for h in range(X_UNITS):
                count_x(0, h)
                if h - 2 in FIRST_BEHIND:
                    u = FIRST_BEHIND.index(h - 2)
                    split_block(dve, False, u, u, 0)
            for b in range(B):
                dve.wait_ge(x_counted, (b + 1) * X_UNITS)
                for c in range(NC):
                    last = nc.vector.bn_aggr(channel[:, c, :], stats[:, c, :, :])
                last.then_inc(channel_ready, 1)
                dve.wait_ge(mean_summed, b + 1)
                nc.vector.tensor_copy(group_mean[:, :], bank[6][:, 0:NC]).then_inc(dve_step, 1)
                dve.wait_ge(dve_step, 4 * b + 1)
                nc.vector.tensor_tensor(centre[:, :], channel[:, :, 0], group_mean[:, :],
                                        ALU.subtract).then_inc(dve_step, 1)
                dve.wait_ge(dve_step, 4 * b + 2)
                nc.vector.tensor_tensor(square[:, :], centre[:, :], centre[:, :],
                                        ALU.mult).then_inc(dve_step, 1)
                dve.wait_ge(dve_step, 4 * b + 3)
                nc.vector.tensor_tensor(spread[:, :], square[:, :], channel[:, :, 1],
                                        ALU.add).then_inc(spread_ready, 1)
                dve.wait_ge(var_summed, b + 1)
                nc.vector.tensor_scalar(group_var[:, :], bank[7][:, 0:NC], GN_EPS, None,
                                        ALU.add).then_inc(var_ready, 1)
                dve.wait_ge(deviation_ready, b + 1)
                nc.vector.reciprocal(inverse[:, :], deviation[:, :]).then_inc(dve_step, 1)
                dve.wait_ge(dve_step, 4 * b + 4)
                reached(dve, tile_done, tile(b, 0, 0))
                for h in range(X_UNITS):
                    n, c = x_unit(b, True, h), h // 2
                    dve.wait_ge(x_loaded[n % X_SLOTS], 16 * (n // X_SLOTS + 1))
                    nc.vector.tensor_scalar(xs[:, n % X_SLOTS, :], xs[:, n % X_SLOTS, :],
                                            group_mean[:, c:c + 1], inverse[:, c:c + 1], ALU.subtract,
                                            ALU.mult).then_inc(x_normal, 1)
                    if h and h % 2 == 0:
                        low_x(dve, b, h - 1, x_low_dve)
                    if h - 1 in V_BEHIND:
                        split_v(dve, False, b, LB, (V_BEHIND.index(h - 1),))
                low_x(dve, b, X_UNITS - 1, x_low_dve)
                weights_and_tiles(dve, False, b)



STAGES = T // NQ
S_TILES = 40
M_UNITS = 40
AHEAD = 3
M_AHEAD = 23
PAIRS = G_HEADS // 2
RAW_UNITS = 5
SPLITS = 2 * RAW_UNITS
RR = T // 16
JP = 8
OP_PIECES = 6
DIAGONAL_SLOT = {2: 4, 3: 17, 0: 22, 1: 30}
SHIFT_SLOT = {2: 6, 3: 19, 0: 24, 1: 32}
HIGH_SLOT = {0: 0, 1: 1, 2: 2, 3: 3, 4: 8, 5: 9, 6: 11, 7: 14, 8: 15, 9: 16}
K2_SLOT = {4: 8, 5: 9, 6: 10, 7: 13}
LOW_SLOT = {n: 2 * n + 1 for n in HIGH_SLOT}
LEAVE_SLOT = {3: 0, 0: 7, 1: 12, 2: 24}
DIVIDE_SLOT = {3: 1, 0: 9, 1: 14, 2: 26}
ROUND_SLOT = {("high", 0): 4, ("high", 1): 5, ("low", 0): 6, ("low", 1): 7}
OP_SLOT = {0: 9, 1: 10, 2: 11, 3: 15, 4: 16, 5: 17}
ADD_SLOT = {0: 13, 1: 19}
LOW_DVE = (3, 8)
WO_UNITS = 16
WO_SLOT = {w: 12 + 3 * w // 2 for w in range(WO_UNITS)}
HIGH_DVE = ()


def score_tile(kind, t):
    s = 0
    while t >= 4 * (s + 1):
        t -= 4 * (s + 1)
        s += 1
    over = t - 4 * s
    qb, j = (s, t) if kind == LB else (STAGES - 1 - s, TOK - 1 - t)
    if over < 0:
        return s, t, qb, j, 0, NQ, None
    if kind == LB:
        return s, t, qb, j, over * P, NQ - over * P, over * P
    return s, t, qb, j, 0, NQ - over * P, NQ - (over + 1) * P


def max_unit(kind, n):
    s = 0
    while n >= 4 * (s + 1):
        n -= 4 * (s + 1)
        s += 1
    r, m = n // (s + 1), n % (s + 1)
    keys = (4 * s + r + 1) * P
    lo, hi = m * NQ, min(keys, (m + 1) * NQ)
    diagonal = keys - P if hi == keys else None
    if kind == LB:
        return s, r, m, 4 * s + r, lo, hi - lo, diagonal
    return (s, r, m, TOK - 1 - 4 * s - r, T - hi, hi - lo,
            None if diagonal is None else T - keys)


def slots(has_next, has_before):
    plan = []
    for t in range(S_TILES):
        for step, n in (("max", t + M_AHEAD), ("scores", t + AHEAD)):
            if has_next or n < 40:
                plan.append((step, n >= 40, n % 40))
        for step, at_slot in (("diagonal", DIAGONAL_SLOT), ("shift", SHIFT_SLOT)):
            for s, at in at_slot.items():
                if at == t and (has_next or s >= 2):
                    plan.append((step, s < 2, s))
        for s, at in DIVIDE_SLOT.items():
            for step, later in (("invert", 0), ("spread", 1), ("divide", 2)):
                if at + later == t and (has_before or s < 3):
                    plan.append((step, False, s))
        for s, at in LEAVE_SLOT.items():
            if at == t and (has_before or s < 3):
                plan.append(("leave", False, s))
        for (part, half), at in ROUND_SLOT.items():
            if at == t and has_before:
                plan.append(("round " + part, False, half))
        for step, at_slot in (("k2 high", K2_SLOT), ("split high", HIGH_SLOT), ("split low", LOW_SLOT)):
            for n, at in at_slot.items():
                if at == t and has_next:
                    plan.append((step, True, n))
        for n, at in OP_SLOT.items():
            if at == t and has_before:
                plan.append(("project", False, n))
        for half, at in ADD_SLOT.items():
            if at == t and has_before:
                plan.append(("add", False, half))
        for w, at in WO_SLOT.items():
            if at == t and not has_before:
                plan.append(("weights", False, w))
        plan.append(("values", False, t))
    return plan


def prologue():
    return ([(step, False, n) for n in range(SPLITS) for step in ("k2 high", "split high", "split low")
             if step != "k2 high" or n in K2_SLOT]
            + [("max", False, n) for n in range(4)] + [("diagonal", False, 0), ("shift", False, 0)]
            + [("max", False, n) for n in range(4, 12)] + [("diagonal", False, 1),
               ("shift", False, 1)]
            + [("max", False, n) for n in range(12, M_AHEAD)]
            + [("scores", False, t) for t in range(AHEAD)])


def attend(nc, x_res, wo, qk_s, v_s, out):
    with ExitStack() as ctx:
        def sb(name, shape, dt=F32):
            return ctx.enter_context(nc.sbuf_tensor(name, shape, dt))

        def sem(name):
            return ctx.enter_context(nc.semaphore(name))

        q1 = sb("q1", [P, 2, T], F32R)
        q2 = sb("q2", [P, 2, T], F32R)
        k1 = sb("k1", [P, 2, T], F32R)
        k2 = sb("k2", [P, 2, T], F32R)
        VC = 3 * E + 1
        v = sb("v", [P, 2, TOK, VC], F32R)
        raw = sb("raw", [P, 2, HALF])
        probs = sb("probs", [P, 4, NQ])
        p_high = sb("p_high", [P, 4, NQ], F32R)
        p_low = sb("p_low", [P, 4, NQ], F32R)
        acc_s = sb("acc_s", [P, NQ])
        inv_c = sb("inv_c", [E, NQ // 32])
        inv = sb("inv", [E, NQ])
        o_full = sb("o_full", [P, JP, RR])
        o_high = sb("o_high", [P, JP, RR], F32R)
        o_low = sb("o_low", [P, JP, RR], F32R)
        wo_h = sb("wo_h", [P, JP, D], F32R)
        wo_l = sb("wo_l", [P, JP, D], F32R)
        res = sb("res", [P, 2, NQ])
        part_max = sb("part_max", [P, 2, 4, 4])
        minus_max = sb("minus_max", [P, 2, 4], F32R)
        eye = sb("eye", [P, P])
        diagonal = sb("diagonal", [P, 4, P], F32R)
        eye_b = sb("eye_b", [P, P], BF16)
        below = sb("below", [P, P], BF16)
        beyond = sb("beyond", [P, P], BF16)

        def bank(name):
            return ctx.enter_context(nc.psum_tensor(name, [P, NQ], F32))

        scores = [bank(f"scores{n}") for n in range(2)]
        max_bank = [bank(f"max{n}") for n in range(2)]
        acc = [bank(f"acc{n}") for n in range(2)]
        side = bank("side")
        rows_bank = bank("rows")

        raw_loaded = [sem(f"raw_loaded{n}") for n in range(2)]
        wo_loaded = [sem(f"wo_loaded{n}") for n in range(2)]
        wo_high = sem("wo_high")
        wo_split = sem("wo_split")
        res_loaded = sem("res_loaded")
        cleared = sem("cleared")
        eye_made = sem("eye_made")
        consts = sem("consts")
        act_split = sem("act_split")
        low_split = sem("low_split")
        max_scored = sem("max_scored")
        max_masked = sem("max_masked")
        max_read = sem("max_read")
        max_ready = sem("max_ready")
        diagonal_made = sem("diagonal_made")
        row_ready = sem("row_ready")
        shift_ready = sem("shift_ready")
        scored = sem("scored")
        exp_done = sem("exp_done")
        high_act = sem("high_act")
        high_dve = sem("high_dve")
        low_pool = sem("low_pool")
        low_dve = sem("low_dve")
        weighed = sem("weighed")
        acc_copied = sem("acc_copied")
        divide_step = sem("divide_step")
        o_ready = sem("o_ready")
        o_high_ready = sem("o_high_ready")
        o_low_ready = sem("o_low_ready")
        projected = sem("projected")
        added = sem("added")
        stored = sem("stored")

        def pairs(eng, body):
            body(0, LB, LB)
            with eng.Fori(1, PAIRS // 2 - 1) as i:
                body(i, LB, LB)
            body(PAIRS // 2 - 1, LB, LA)
            body(PAIRS // 2, LA, LA)
            with eng.Fori(PAIRS // 2 + 1, PAIRS - 1) as i:
                body(i, LA, LA)
            body(PAIRS - 1, LA, None)

        def heads(eng, do):
            for step, _, n in prologue():
                do(step, LB, 0, 0, n)

            def pair(i, kind, then):
                for p in range(2):
                    of = kind if p == 0 else then
                    following = (i, 1) if p == 0 else (i + 1, 0)
                    has_before = p == 1 or not isinstance(i, int) or i > 0
                    for step, later, n in slots(of is not None, has_before):
                        if later:
                            do(step, of, *following, n)
                        else:
                            do(step, kind, i, p, n)

            pairs(eng, pair)
            for step in ("leave", "invert", "spread", "divide"):
                do(step, LA, PAIRS, 0, 3)
            for part, half in ROUND_SLOT:
                do("round " + part, None, PAIRS, 0, half)
            for half in range(2):
                for n in range(3 * half, 3 * half + 3):
                    do("project", None, PAIRS, 0, n)
                do("add", None, PAIRS, 0, half)

        def count(i, p, per_head, n):
            return i * (2 * per_head) + (p * per_head + n)

        def taken(members, n):
            return n // 4 * len(members) + sum(m <= n % 4 for m in members)

        HIGH_ACT = tuple(m for m in range(4) if m not in HIGH_DVE)

        def wait_one(eng, sem, members, i, p, n):
            reached(eng, sem, count(i, p, S_TILES // 4 * len(members), taken(members, n)))

        def wait_high(eng, i, p, n):
            if n % 4 in HIGH_DVE:
                wait_one(eng, high_dve, HIGH_DVE, i, p, n)
            else:
                wait_one(eng, high_act, HIGH_ACT, i, p, n)

        def wait_low(eng, i, p, n):
            reached(eng, low_dve, count(i, p, S_TILES, n + 1))
            reached(eng, low_pool, count(i, p, S_TILES, n + 1))

        def low_part(eng, done, kind, i, p, n):
            cols = score_tile(kind, n % S_TILES)[5]
            mine = cols * LOW_DVE[0] // LOW_DVE[1]
            part = slice(0, mine) if done is low_dve else slice(mine, cols)
            wait_high(eng, i, p, n)
            reached(eng, weighed, count(i, p, S_TILES, n - 3))
            eng.tensor_tensor(p_low[:, n % 4, part], probs[:, n % 4, part],
                              p_high[:, n % 4, part].bitcast(F32), ALU.subtract).then_inc(done, 1)

        def first_head(i, p):
            return isinstance(i, int) and (i, p) == (0, 0)

        def put_diagonal(eng, i, p, n):
            eng.wait_ge(max_ready, count(i, p, STAGES, n + 1))
            reached(eng, row_ready, count(i, p, STAGES, n))
            eng.tensor_tensor(diagonal[:, :, :],
                              eye[:, :].rearrange("p (a q) -> p a q", a=1).broadcast_to([P, 4, P]),
                              minus_max[:, n % 2, :].rearrange("p (r a) -> p r a", a=1)
                              .bitcast(F32).broadcast_to([P, 4, P]), ALU.mult).then_inc(diagonal_made, 1)

        def split_low(eng, p, slot, u, h):
            src = slice(h * NQ, (h + 1) * NQ)
            cols = slice((u % 2) * HALF + h * NQ, (u % 2) * HALF + (h + 1) * NQ)
            if u < 2:
                ins = eng.tensor_tensor(q2[0:E, p, cols], raw[0:E, slot, src],
                                        q1[0:E, p, cols].bitcast(F32), ALU.subtract)
            elif u < 4:
                low = k1[E:P, p, cols]
                ins = eng.tensor_tensor(low, raw[E:P, slot, src], low.bitcast(F32), ALU.subtract)
            else:
                js = slice(h * TOK // 2, (h + 1) * TOK // 2)
                ins = eng.tensor_tensor(
                    v[:, p, js, 2 * E:3 * E], raw[:, slot, src].rearrange("p (t e) -> p t e", e=E),
                    v[:, p, js, 0:E].bitcast(F32), ALU.subtract)
            ins.then_inc(low_split, 1)

        block = ctx.enter_context(nc.Block())

        @block.sync
        def _(sp):
            def load_raw(i, p, kind):
                row = i + kind * PAIRS // 2
                for u in range(RAW_UNITS):
                    slot = (p * RAW_UNITS + u) % 2
                    reached(sp, act_split, count(i, p, SPLITS, 2 * u - 2))
                    reached(sp, low_split, count(i, p, SPLITS, 2 * u - 2))
                    if u < 4:
                        src = qk_s[bass.ds(row + (u // 2) * (B * 4), 1), p * E:(p + 1) * E,
                                   (u % 2) * HALF:(u % 2 + 1) * HALF].rearrange("a e t -> (a e) t")
                        for copy in range(2):
                            sp.dma_start(raw[copy * E:(copy + 1) * E, slot, :], src).then_inc(raw_loaded[slot], 16)
                    else:
                        src = v_s[bass.ds(2 * i + p, 1)].rearrange("a p t e -> (a p) (t e)")
                        for half in range(2):
                            cols = slice(half * NQ, (half + 1) * NQ)
                            sp.dma_start(raw[:, slot, cols], src[:, cols]).then_inc(raw_loaded[slot], 16)

            def residual(g):
                reached(sp, stored, g * 16)
                sp.dma_start(res[:, :, :].rearrange("p a n -> p (a n)"),
                             x_res[bass.ds(g, 1)].rearrange("a p d -> (a p) d")).then_inc(res_loaded, 16)

            def rows_out(g):
                sp.wait_ge(added, g * 2 + 2)
                sp.dma_start(out[bass.ds(g, 1)].rearrange("a p d -> (a p) d"),
                             res[:, :, :].rearrange("p a n -> p (a n)")).then_inc(stored, 16)

            load_raw(0, 0, LB)

            def pair(i, kind, then):
                for p in range(2):
                    of = kind if p == 0 else then
                    if of is not None:
                        load_raw(*((i, 1) if p == 0 else (i + 1, 0)), of)
                    if isinstance(i, int) and i == 0 and p == 0:
                        for w in range(WO_UNITS):
                            reached(sp, wo_split, w - 1)
                            sp.dma_start(res[:, w % 2, :],
                                         wo[:, w // 2, (w % 2) * NQ:(w % 2 + 1) * NQ]).then_inc(wo_loaded[w % 2], 16)
                        sp.wait_ge(wo_split, WO_UNITS)
                        residual(0)
                    if p == 1 or not isinstance(i, int) or i > 0:
                        before = 2 * i + (p - 1)
                        rows_out(before)
                        residual(before + 1)

            pairs(sp, pair)
            rows_out(G_HEADS - 1)
            sp.wait_ge(stored, 16 * G_HEADS)

        @block.gpsimd
        def _(pool):
            nc.gpsimd.memset(eye[:, :], 0.0).then_inc(eye_made, 1)
            nc.gpsimd.memset(below[:, :], 0.0).then_inc(eye_made, 1)
            nc.gpsimd.memset(beyond[:, :], 0.0).then_inc(eye_made, 1)
            pool.wait_ge(eye_made, 3)
            nc.gpsimd.affine_select(out=eye[:, :], in_=eye[:, :], compare_op=ALU.not_equal, fill=1.0,
                                    base=0, pattern=[[-1, P]], channel_multiplier=1).then_inc(eye_made, 1)
            nc.gpsimd.affine_select(out=below[:, :], in_=below[:, :], compare_op=ALU.is_ge, fill=MASKED,
                                    base=0, pattern=[[1, P]], channel_multiplier=-1).then_inc(consts, 1)
            nc.gpsimd.affine_select(out=beyond[:, :], in_=beyond[:, :], compare_op=ALU.is_ge, fill=MASKED,
                                    base=0, pattern=[[-1, P]], channel_multiplier=1).then_inc(consts, 1)

            pool.wait_ge(consts, 2)
            for p in range(2):
                nc.gpsimd.memset(q2[E:P, p, :].bitcast(F32), 0.0).then_inc(cleared, 1)
                nc.gpsimd.memset(k2[E:P, p, :].bitcast(F32), 0.0).then_inc(cleared, 1)
            pool.wait_ge(cleared, 4)
            for p in range(2):
                nc.gpsimd.memset(k2[E:E + 1, p, :].bitcast(F32), 1.0).then_inc(cleared, 1)
            pool.wait_ge(cleared, 6)
            for p in range(2):
                nc.gpsimd.memset(v[:, p, :, E:2 * E].bitcast(F32), 1.0).then_inc(cleared, 1)
                nc.gpsimd.memset(v[:, p, :, 3 * E:VC].bitcast(F32), 0.0).then_inc(cleared, 1)

            def do(step, kind, i, p, n):
                if step == "split low" and not first_head(i, p):
                    u, h = n // 2, n % 2
                    slot = (p * RAW_UNITS + u) % 2
                    pool.wait_ge(act_split, count(i, p, SPLITS, n + 1))
                    reached(pool, low_split, count(i, p, SPLITS, n))
                    reached(pool, low_pool, count(i, p, S_TILES, LOW_SLOT[n] + AHEAD - S_TILES + 1))
                    split_low(pool, p, slot, u, h)
                    pool.wait_ge(low_split, count(i, p, SPLITS, n + 1))
                elif step == "scores":
                    low_part(pool, low_pool, kind, i, p, n)

            heads(pool, do)

        @block.scalar
        def _(act):
            def do(step, kind, i, p, n):
                if step in ("split high", "k2 high"):
                    u, h = n // 2, n % 2
                    slot = (p * RAW_UNITS + u) % 2
                    act.wait_ge(raw_loaded[slot], 32 * (i * RAW_UNITS + ((p * RAW_UNITS + u) // 2 + 1)))
                    reached(act, weighed, count(i, p, S_TILES, -S_TILES))
                    src = slice(h * NQ, (h + 1) * NQ)
                    cols = slice((u % 2) * HALF + h * NQ, (u % 2) * HALF + (h + 1) * NQ)
                    if step == "k2 high":
                        nc.scalar.activation(k2[0:E, p, cols], raw[0:E, slot, src], ACT.Copy)
                    elif u < 4:
                        nc.scalar.activation((q1 if u < 2 else k1)[:, p, cols], raw[:, slot, src],
                                             ACT.Copy).then_inc(act_split, 1)
                    else:
                        js = slice(h * TOK // 2, (h + 1) * TOK // 2)
                        nc.scalar.activation(v[:, p, js, 0:E], raw[:, slot, src].rearrange(
                            "p (t e) -> p t e", e=E), ACT.Copy).then_inc(act_split, 1)
                elif step == "shift":
                    act.wait_ge(row_ready, count(i, p, STAGES, n + 1))
                    qb = n if kind == LB else STAGES - 1 - n
                    nc.scalar.activation(q2[E:E + 1, p, qb * NQ:(qb + 1) * NQ], side[E:E + 1, :],
                                         ACT.Copy).then_inc(shift_ready, 1)
                elif step == "scores":
                    cols = score_tile(kind, n)[5]
                    act.wait_ge(scored, count(i, p, S_TILES, n + 1))
                    wait_low(act, i, p, n - 4)
                    nc.scalar.activation(probs[:, n % 4, 0:cols], scores[n % 2][:, 0:cols], ACT.Exp,
                                         scale=SCALE).then_inc(exp_done, 1)
                    if n % 4 in HIGH_ACT:
                        reached(act, weighed, count(i, p, S_TILES, n - 3))
                        nc.scalar.activation(p_high[:, n % 4, 0:cols], scores[n % 2][:, 0:cols], ACT.Exp,
                                             scale=SCALE).then_inc(high_act, 1)
                elif step == "leave":
                    tiles = -1 if n == 3 else 2 * (n + 1) * (n + 2) - 1
                    act.wait_ge(weighed, count(i, p, S_TILES, tiles + 1))
                    reached(act, o_ready, count(i, p, STAGES, -1 if n == 3 else n))
                    nc.scalar.activation(acc_s[:, :], acc[n % 2][:, :], ACT.Copy).then_inc(acc_copied, 1)
                elif step == "weights":
                    act.wait_ge(wo_loaded[n % 2], 16 * (n // 2 + 1))
                    nc.scalar.activation(wo_h[:, n // 2, (n % 2) * NQ:(n % 2 + 1) * NQ], res[:, n % 2, :],
                                         ACT.Copy).then_inc(wo_high, 1)
                elif step == "round high":
                    act.wait_ge(o_ready, count(i, p, STAGES, 0))
                    reached(act, projected, count(i, p, 2, -2))
                    js = slice(n * JP // 2, (n + 1) * JP // 2)
                    nc.scalar.activation(o_high[:, js, :], o_full[:, js, :], ACT.Copy).then_inc(o_high_ready, 1)

            heads(act, do)

        @block.vector
        def _(dve):
            dve.wait_ge(eye_made, 4)
            dve.wait_ge(consts, 2)
            nc.vector.tensor_copy(eye_b[:, :], eye[:, :]).then_inc(consts, 1)
            def divided(i, p, n):
                return count(i, p, 3 * STAGES, 3 * n) if n < 3 else count(i, p, 3 * STAGES, -3)

            def div_kind(kind, i, p, n):
                if n == 3 and p == 0 and isinstance(i, int) and i == PAIRS // 2:
                    return LB
                return kind

            def both_parts(kind, i, p, n):
                if n % 4 in HIGH_DVE:
                    cols = score_tile(kind, n % S_TILES)[5]
                    dve.wait_ge(exp_done, count(i, p, S_TILES, n + 1))
                    reached(dve, weighed, count(i, p, S_TILES, n - 3))
                    nc.vector.tensor_copy(p_high[:, n % 4, 0:cols],
                                          probs[:, n % 4, 0:cols]).then_inc(high_dve, 1)
                low_part(dve, low_dve, kind, i, p, n)

            def do(step, kind, i, p, n):
                if step == "diagonal":
                    put_diagonal(dve, i, p, n)
                elif step == "max":
                    s, r, m, _, key, cols, square = max_unit(kind, n)
                    dve.wait_ge(max_scored, count(i, p, M_UNITS, n + 1))
                    if square is not None:
                        own = max_bank[n % 2][:, square - key:square - key + P]
                        nc.vector.tensor_tensor(own, own, (beyond if kind == LB else below)[:, :],
                                                ALU.add).then_inc(max_masked, 1)
                        dve.wait_ge(max_masked, count(i, p, 4 * STAGES, 4 * s + r + 1))
                    at = r if kind == LB else 3 - r
                    nc.vector.tensor_reduce(part_max[:, s % 2, at, m:m + 1], max_bank[n % 2][:, 0:cols],
                                            AX.X, ALU.max).then_inc(max_read, 1)
                    if r == 3 and m == s:
                        dve.wait_ge(max_read, count(i, p, M_UNITS, n + 1))
                        nc.vector.tensor_reduce(minus_max[:, s % 2, :], part_max[:, s % 2, :, 0:s + 1],
                                                AX.X, ALU.max, negate=True).then_inc(max_ready, 1)
                elif step == "scores":
                    if n or p or not isinstance(i, int) or i:
                        both_parts(kind, i, p, n - 1)
                elif step == "values" and n == S_TILES - 1 - AHEAD:
                    if isinstance(i, int) and (i, p) == (PAIRS - 1, 1):
                        both_parts(kind, i, p, S_TILES - 1)
                elif step == "split low" and first_head(i, p):
                    dve.wait_ge(act_split, n + 1)
                    reached(dve, low_split, n)
                    split_low(dve, p, n // 2 % 2, n // 2, n % 2)
                elif step == "weights":
                    part = (slice(None), n // 2, slice((n % 2) * NQ, (n % 2 + 1) * NQ))
                    dve.wait_ge(wo_high, n + 1)
                    nc.vector.tensor_tensor(wo_l[part], res[:, n % 2, :], wo_h[part].bitcast(F32),
                                            ALU.subtract).then_inc(wo_split, 1)
                elif step == "invert":
                    done = count(i, p, STAGES, n + 1) if n < 3 else count(i, p, STAGES, 0)
                    steps = divided(i, p, n)
                    dve.wait_ge(acc_copied, done)
                    nc.vector.transpose(inv[:, :], acc_s[E:P, :]).then_inc(divide_step, 1)
                    dve.wait_ge(divide_step, steps + 1)
                    nc.vector.reciprocal(inv_c[:, :], inv[:, :].rearrange("e (b c) -> e b c", c=32)[:, :, 0]
                                         ).then_inc(divide_step, 1)
                elif step == "spread":
                    steps = divided(i, p, n)
                    dve.wait_ge(divide_step, steps + 2)
                    nc.vector.transpose(inv[:, :], inv_c[:, :].rearrange("e (b c) -> e b c", c=1)
                                        .broadcast_to([E, NQ // 32, 32])).then_inc(divide_step, 1)
                elif step == "divide":
                    dve.wait_ge(divide_step, divided(i, p, n) + 3)
                    if n == 0:
                        reached(dve, o_low_ready, count(i, p, 2, 0))
                    qb = n if div_kind(kind, i, p, n) == LB else STAGES - 1 - n
                    rows = slice(qb * NQ // 16, (qb + 1) * NQ // 16)
                    for a in range(2):
                        sums, by = (x.rearrange("e (r j a) -> e a j r", j=JP, a=2)[:, a]
                                    for x in (acc_s[0:E, :], inv[:, :]))
                        last = nc.vector.tensor_tensor(o_full[a * E:(a + 1) * E, :, rows], sums, by, ALU.mult)
                    last.then_inc(o_ready, 1)
                elif step == "round low":
                    dve.wait_ge(o_high_ready, count(i, p, 2, n - 1))
                    js = slice(n * JP // 2, (n + 1) * JP // 2)
                    nc.vector.tensor_tensor(o_low[:, js, :], o_full[:, js, :], o_high[:, js, :].bitcast(F32),
                                            ALU.subtract).then_inc(o_low_ready, 1)
                elif step == "add":
                    half = n
                    dve.wait_ge(projected, count(i, p, 2, half - 1))
                    dve.wait_ge(res_loaded, 16 * count(i, p, 1, 0))
                    nc.vector.tensor_tensor(res[:, half, :], rows_bank[:, :], res[:, half, :],
                                            ALU.add).then_inc(added, 1)

            heads(dve, do)

        @block.tensor
        def _(pe):
            pe.wait_ge(consts, 3)

            def do(step, kind, i, p, n):
                if step == "max":
                    _, _, _, qc, key, cols, _ = max_unit(kind, n)
                    if n == 0:
                        pe.wait_ge(low_split, count(i, p, SPLITS, 8))
                    reached(pe, max_read, count(i, p, M_UNITS, n - 1))
                    to = max_bank[n % 2]
                    nc.tensor.matmul(to[:, 0:cols], q1[:, p, qc * P:(qc + 1) * P],
                                     k1[:, p, key:key + cols], start=True, stop=True).then_inc(max_scored, 1)
                elif step == "shift":
                    if first_head(i, p) and n == 0:
                        pe.wait_ge(cleared, 10)
                    pe.wait_ge(diagonal_made, count(i, p, STAGES, n + 1))
                    reached(pe, shift_ready, count(i, p, STAGES, n))
                    nc.tensor.matmul(side[:, :], v[:, 0, 0, E:E + 1].broadcast_to([P, P]), diagonal[:, :, :],
                                     start=True, stop=True).then_inc(row_ready, 1)
                elif step == "scores":
                    s, at, qb, j, col, cols, square = score_tile(kind, n)
                    if at == 0:
                        pe.wait_ge(shift_ready, count(i, p, STAGES, s + 1))
                    if (n - 2) % 4 in HIGH_ACT:
                        wait_one(pe, high_act, HIGH_ACT, i, p, n - 2)
                    else:
                        reached(pe, exp_done, count(i, p, S_TILES, n - 1))
                    keys = slice(j * P, (j + 1) * P)
                    queries = slice(qb * NQ + col, qb * NQ + col + cols)
                    to = scores[n % 2]
                    nc.tensor.matmul(to[:, 0:cols], k1[:, p, keys], q1[:, p, queries], start=True, stop=False)
                    if square is not None:
                        nc.tensor.matmul(to[:, square - col:square - col + P], eye_b[:, :],
                                         (below if kind == LB else beyond)[:, :], start=False, stop=False)
                    nc.tensor.matmul(to[:, 0:cols], k2[:, p, keys], q2[:, p, queries],
                                     start=False, stop=True).then_inc(scored, 1)
                elif step == "values":
                    s, at, _, j, col, cols, _ = score_tile(kind, n)
                    first, final = at == 0, at == 4 * (s + 1) - 1
                    if n == 0:
                        pe.wait_ge(low_split, count(i, p, SPLITS, SPLITS))
                    if first:
                        reached(pe, acc_copied, count(i, p, STAGES, s - 1))
                    wait_low(pe, i, p, n)
                    high, low = p_high[:, n % 4, 0:cols], p_low[:, n % 4, 0:cols]
                    sums = acc[s % 2]
                    nc.tensor.matmul(sums[:, col:col + cols], v[:, p, j, 0:P], high, start=first, stop=False,
                                     skip_group_check=True)
                    nc.tensor.matmul(sums[0:E + 1, col:col + cols], v[:, p, j, P:VC], high, start=False,
                                     stop=False, skip_group_check=True)
                    nc.tensor.matmul(sums[:, col:col + cols], v[:, p, j, 0:P], low, start=False, stop=final,
                                     skip_group_check=True).then_inc(weighed, 1)
                elif step == "project":
                    half, third = n // 3, n % 3
                    if n == 0:
                        pe.wait_ge(o_low_ready, count(i, p, 2, 0))
                    if third == 0:
                        reached(pe, added, count(i, p, 2, half - 2))
                    cols = slice(half * NQ, (half + 1) * NQ)
                    products = [(j, o, w) for j in range(JP)
                                for o, w in ((o_high, wo_h), (o_high, wo_l), (o_low, wo_h))]
                    for k in range(third * 8, third * 8 + 8):
                        j, o, w = products[k]
                        last = nc.tensor.matmul(rows_bank[:, :], o[:, j, :], w[:, j, cols],
                                                start=(k == 0), stop=(k == 23))
                    if third == 2:
                        last.then_inc(projected, 1)

            heads(pe, do)


def build(nc, xT, x_res, wqk, wv, wo, qk_s, v_s, out):
    project(nc, xT, wqk, wv, qk_s, v_s)
    attend(nc, x_res, wo, qk_s, v_s, out)


def kernel(**inputs):
    import numpy as np
    import concourse.bacc as bacc
    from concourse.bass_utils import run_bass_kernel_spmd as run

    def f32(a):
        return np.asarray(a)

    nc = bacc.Bacc("TRN2", target_bir_lowering=False, num_devices=1)
    x = f32(inputs["x"])
    tokens = x.reshape(B, T, D)
    weights = {w: f32(inputs[f"L0_conv_{w}"]) for w in
               ("Wq_lb", "Wk_lb", "Wv_lb", "Wq_la", "Wk_la", "Wv_la", "Wo")}
    qk = np.stack([weights[w].reshape(4, P, NC, P) for w in ("Wq_lb", "Wk_lb", "Wq_la", "Wk_la")])
    v = np.stack([weights[w].reshape(NQ, V_RAWS, 2, P) for w in ("Wv_lb", "Wv_la")])
    arrays = {
        "xT": tokens.transpose(0, 2, 1).reshape(B, NC, P, T),
        "x_res": tokens.reshape(B, KINDS, HEADS, P, D).transpose(1, 0, 2, 3, 4).reshape(G_HEADS, P, D),
        "wqk": qk.transpose(0, 1, 4, 3, 2).reshape(BLOCKS, P, D),
        "wv": v.transpose(0, 2, 4, 3, 1).reshape(KINDS, V_RAWS, P, D),
        "wo": weights["Wo"].reshape(D, JP, P).transpose(2, 1, 0),
    }
    arrays = {k: np.ascontiguousarray(a) for k, a in arrays.items()}
    ins = {k: nc.dram_tensor(k, a.shape, F32, kind="ExternalInput").ap() for k, a in arrays.items()}
    qk_s = nc.dram_tensor("qk_s", (G_HEADS, P, T), F32, kind="Internal").ap()
    v_s = nc.dram_tensor("v_s", (G_HEADS, P, TOK, E), F32, kind="Internal").ap()
    out = nc.dram_tensor("out", (G_HEADS, P, D), F32, kind="ExternalOutput").ap()
    build(nc, ins["xT"], ins["x_res"], ins["wqk"], ins["wv"], ins["wo"], qk_s, v_s, out)
    result = run(nc, [arrays], core_ids=[0])
    rows = result.results[0]["out"].reshape(KINDS, B, HEADS, P, D).transpose(1, 0, 2, 3, 4)
    return rows.reshape(x.shape)
```
